# Optimizing a Trainium2 kernel written in Bass

```python
import numpy as np
import jax
import jax.numpy as jnp

def _softmax(x, axis=-1):
    return jax.nn.softmax(x, axis=axis)

def _gelu(x):
    return jax.nn.gelu(x, approximate=True)

def _silu(x):
    return jax.nn.silu(x)

def _sigmoid(x):
    return jax.nn.sigmoid(x)

def _layernorm(x, axis=-1, eps=1e-05):
    m = jnp.mean(x, axis=axis, keepdims=True)
    v = jnp.var(x, axis=axis, keepdims=True)
    return (x - m) / jnp.sqrt(v + eps)

def _scatter_add(tgt, idx, src, axis=0):
    return tgt.at[idx].add(src)

def _segment_sum(src, seg, n):
    return jax.ops.segment_sum(src, seg, n)
kernel_name = 'mk_adj_ffn_d1_adj_r2_1264e5'

def setup_inputs(seed: int=0):
    np.random.seed(seed)
    _w = jnp.asarray

    def _rec_inputs():
        import jax
        import jax.numpy as jnp
        _gk = jax.random.key(seed)
        x = -0.0002928 + 1 * jax.random.normal(jax.random.fold_in(_gk, 1), (4096, 256), jnp.float32)
        _w = (1.0 + jnp.arange(4096, dtype=jnp.float32)) ** (-0.5)
        _w = _w / _w.mean()
        _pij = jnp.clip(0.00390625 * _w[:, None] * _w[None, :], 0.0, 1.0)
        _a = jax.random.uniform(jax.random.fold_in(_gk, 2), (4096, 4096)) < _pij
        _a = jnp.logical_or(_a, jnp.swapaxes(_a, -1, -2))
        _a = jnp.logical_or(_a, jnp.eye(4096, dtype=bool))
        _af = _a.astype(jnp.float32)
        _af = _af * jax.random.uniform(jax.random.fold_in(_gk, 3), (4096, 4096), jnp.float32, 0.05, 5.41998)
        adj = _af
        return (x, adj)
    x, adj = _rec_inputs()

    def _L0_gnn_setup():
        import jax, jax.numpy as jnp
        import numpy as np
        N = 4096
        D = 256
        EPS = 1e-12
        key = jax.random.key(seed)
        k1, k2 = jax.random.split(key)
        cur = jax.random.normal(k1, (N, D), dtype=jnp.float32)
        incidence_m = jax.random.normal(k2, (N, N), dtype=jnp.float32)
        return {'cur': cur, 'incidence_m': incidence_m}
    _L0_gnn_all = _L0_gnn_setup()
    _L0_gnn_in = {k: v for k, v in _L0_gnn_all.items() if k in ()}
    del _L0_gnn_all

    def _L0_ffn_setup():
        import jax, jax.numpy as jnp
        import numpy as np
        D = 256
        F = 1024
        E = 8
        K = 2
        B, S = (2, 2048)
        key = jax.random.key(seed)
        ks = jax.random.split(key, 8)
        sd = 1.0 / np.sqrt(D)
        sf = 1.0 / np.sqrt(F)
        return {'x': jax.random.normal(ks[0], (B, S, D), dtype=jnp.float32), 'router_w': jax.random.uniform(ks[1], (D, E), jnp.float32, -sd, sd), 'router_b': jax.random.uniform(ks[2], (E,), jnp.float32, -sd, sd), 'w1': jax.random.uniform(ks[3], (E, D, F), jnp.float32, -sd, sd), 'b1': jax.random.uniform(ks[4], (E, F), jnp.float32, -sd, sd), 'w2': jax.random.uniform(ks[5], (E, F, D), jnp.float32, -sf, sf), 'b2': jax.random.uniform(ks[6], (E, D), jnp.float32, -sf, sf)}
    _L0_ffn_all = _L0_ffn_setup()
    _L0_ffn_in = {k: v for k, v in _L0_ffn_all.items() if k in ('router_w', 'router_b', 'w1', 'b1', 'w2', 'b2')}
    del _L0_ffn_all
    return {'x': x, 'adj': adj, 'L0_ffn_router_w': _L0_ffn_in['router_w'], 'L0_ffn_router_b': _L0_ffn_in['router_b'], 'L0_ffn_w1': _L0_ffn_in['w1'], 'L0_ffn_b1': _L0_ffn_in['b1'], 'L0_ffn_w2': _L0_ffn_in['w2'], 'L0_ffn_b2': _L0_ffn_in['b2']}

def reference(x, adj, L0_ffn_router_w, L0_ffn_router_b, L0_ffn_w1, L0_ffn_b1, L0_ffn_w2, L0_ffn_b2):
    import jax
    import jax.numpy as jnp

    def _L0_gnn_ref(cur, incidence_m):
        import jax, jax.numpy as jnp
        import numpy as np
        N = 4096
        D = 256
        EPS = 1e-12
        mask = incidence_m > 0
        head = jax.lax.stop_gradient(mask.astype(incidence_m.dtype))
        head = head / jnp.maximum(jnp.sqrt(jnp.sum(head * head, axis=-1, keepdims=True)), EPS)
        inc = incidence_m + head
        edge_fea = inc @ cur
        edge_degree = jnp.sum(inc, axis=-1, keepdims=True)
        return edge_fea / edge_degree

    def _L0_ffn_ref(x, router_w, router_b, w1, b1, w2, b2):
        import jax, jax.numpy as jnp
        import numpy as np
        D = 256
        F = 1024
        E = 8
        K = 2
        B, S = (2, 2048)
        orig_shape = x.shape
        flat = x.reshape(-1, orig_shape[-1])
        logits = flat @ router_w + router_b
        gates = jax.nn.softmax(logits, axis=-1)
        top_vals, top_idx = jax.lax.top_k(gates, K)
        top_vals = top_vals / jnp.sum(top_vals, axis=-1, keepdims=True)
        onehot = jax.nn.one_hot(top_idx, E, dtype=flat.dtype)
        comb = jnp.einsum('tk,tke->te', top_vals, onehot)
        hidden = jax.nn.relu(jnp.einsum('td,edf->etf', flat, w1) + b1[:, None, :])
        eout = jnp.einsum('etf,efd->etd', hidden, w2) + b2[:, None, :]
        out = jnp.einsum('te,etd->td', comb, eout)
        return out.reshape(orig_shape)
    x = x + _L0_gnn_ref(_layernorm(x, axis=-1), adj)
    x = x + _L0_ffn_ref(_layernorm(x, axis=-1)[None], L0_ffn_router_w, L0_ffn_router_b, L0_ffn_w1, L0_ffn_b1, L0_ffn_w2, L0_ffn_b2)[0]
    return x

_drawn_inputs = setup_inputs


def setup_inputs(seed=0):
    import zlib

    import numpy as np

    out = dict(_drawn_inputs(seed))
    spreads = {}
    factors = {'L0_ffn_b1': 5.751, 'L0_ffn_b2': 4.614}
    for name, (base, spread) in spreads.items():
        noise = np.random.default_rng([zlib.crc32(name.encode()), seed]).standard_normal(out[name].shape)
        drawn = base * np.exp(spread * noise) if base else spread * noise
        out[name] = jnp.asarray(drawn.astype(out[name].dtype))
    for name, factor in factors.items():
        out[name] = (out[name] * factor).astype(out[name].dtype)
    return out
```

```python
from contextlib import ExitStack

import concourse.bass as bass
from concourse import mybir

ALU = mybir.AluOpType
ACT = mybir.ActivationFunctionType
AX_X = mybir.AxisListType.X
F32 = mybir.dt.float32
F32R = mybir.dt.float32r
F16 = mybir.dt.float16
BF16 = mybir.dt.bfloat16
I32 = mybir.dt.int32
U32 = mybir.dt.uint32
RADD = bass.bass_isa.ReduceOp.add

P = 128
LN_EPS = 1e-5
HEAD_EPS = 1e-12
PAD_ROWS = 2 * P
TINY = 1e-30
W_TOP = 2.0 ** 14
H_TOP = 2.0 ** 15
X_SCALE = 256.0


def is_static(v):
    return isinstance(v, int)


def wait(eng, semaphore, value):
    if is_static(value) and value <= 0:
        return
    eng.wait_ge(semaphore, value)


def gnn_moe_kernel(nc, x, adj, router_w, router_b, w1, b1, w2, b2, out):
    N, D = x.shape
    E, _, F = w1.shape
    DC = D // P
    JC = N // P
    NT = N // P
    RING = 4
    GROUPS = 4
    GJ = JC // GROUPS
    GW = GJ * P
    XCH = 4
    XROW = 2 * D + 2 * E

    ctx = ExitStack()
    with ctx:
        def sb(name, shape, dt, stack=ctx):
            return stack.enter_context(nc.sbuf_tensor(name, shape, dt))

        def ps(name, shape, dt, stack=ctx):
            return stack.enter_context(nc.psum_tensor(name, shape, dt))

        def sem(name):
            return ctx.enter_context(nc.semaphore(name))

        W = F * D // P
        WH = W // 2
        FC = F // P
        TT = 2 * P
        EXPERT_TILES = 2 * N // TT + E - 1
        HALVES = 2 * EXPERT_TILES
        PADS = N + PAD_ROWS

        w_hl = nc.dram_tensor("split_weights", [E, 2, P, 2, W], F16, kind="Internal").ap()
        xtab = nc.dram_tensor("expert_inputs", [N, XROW // 2], U32, kind="Internal").ap()

        logits = sb("logits", [P, NT, E], F32)
        ident = sb("ident", [P, P], F32)
        ident16 = sb("ident16", [P, P], F16)
        w_norm = sb("w_norm", [P, 2, E], F32)
        b_norm = sb("b_norm", [P, E], F32)
        b1t = sb("b1t", [P, E, FC], F32)
        lanes = sb("lanes", [P, P], F32)
        lanes_b = sb("lanes_b", [P, P], BF16)
        lane_col = sb("lane_col", [P, 1], F32)
        order_e = sb("order_e", [P, E], F32)
        tok_hi = sb("tok_hi", [P, 2 * NT], BF16)
        pad_rows = sb("pad_rows", [P, 2], F32)
        earlier = sb("earlier", [P, P], BF16)
        ones_b = sb("ones_b", [P, P], BF16)
        ones_f = sb("ones_f", [P, P], F32)
        ones_row = sb("ones_row", [P, NT * E], F32)

        st2 = ctx.enter_context(ExitStack())
        cur = sb("cur", [P, JC, 2, D], F32R, st2)
        cur32 = cur[:, :, :, :].bitcast(F32)
        adj_t = sb("adj_tiles", [P, RING, N], F32, st2)
        mask = sb("mask", [P, 2, N], BF16, st2)
        inc_hi = sb("inc_hi", [P, 2, GW], F32R, st2)
        inc_lo = sb("inc_lo", [P, 2, GW], F32R, st2)
        stats = sb("stats", [P, XCH, 6], F32, st2)
        mom = sb("mom", [P, 2, XCH, 2], F32, st2)
        sdev = sb("sdev", [P, 2, XCH], F32, st2)
        rstd = sb("rstd", [P, 2, XCH], F32, st2)
        nmr = sb("nmr", [P, 2, XCH], F32, st2)
        eps_c = sb("eps_c", [P, 1], F32, st2)
        rw = sb("rw", [P, DC, E], F32, st2)
        rb = sb("rb", [P, E], F32, st2)
        cnt4 = sb("cnt4", [P, 2, GROUPS], F32, st2)
        cnt = sb("cnt", [P, 2], F32, st2)
        root = sb("root", [P, 2], F32, st2)
        rclip = sb("rclip", [P, 2], F32, st2)
        rinv = sb("rinv", [P, 2], F32, st2)
        deg4 = sb("deg4", [P, 2, GROUPS], F32, st2)
        deg = sb("deg", [P, 2], F32, st2)
        rdeg = sb("rdeg", [P, 2], F32, st2)
        x_res = sb("x_res", [P, 2, D], F32, st2)
        part = sb("part", [P, 2, D], F32, st2)
        x2 = sb("x2", [P, 2, D], F32, st2)
        st_b = sb("st_b", [P, 6], F32, st2)
        mom_b = sb("mom_b", [P, 2], F32, st2)
        sd_b = sb("sd_b", [P, 1], F32, st2)
        sd_s = sb("sd_s", [P, 1], F32, st2)
        rstd_b = sb("rstd_b", [P, 1], F32, st2)
        nmr_b = sb("nmr_b", [P, 1], F32, st2)
        xn = sb("xn", [P, 2, D], F32, st2)
        xnT = sb("xnT", [P, DC, P], F32, st2)
        xhl = sb("xhl", [P, 2, 2, D], F16, st2)

        with ExitStack() as st1:
            x_in = sb("x_in", [P, 4, XCH, D], F32, st1)
            cur_f = sb("cur_f", [P, 2, XCH, D], F32, st1)
        w_in = sb("w_in", [P, 2, W], F32, st2)
        w_parts = sb("w_parts", [P, 2, W], F16, st2)
        w_junk = sb("w_junk", [P, WH], BF16, st2)
        w_sq = sb("w_sq", [P, 2], F32, st2)
        w_sum = sb("w_sum", [P, 1], F32, st2)
        w_tot = sb("w_tot", [P, 1], F32, st2)
        w_root = sb("w_root", [P, 1], F32, st2)
        w_cut = sb("w_cut", [P, 1], F32, st2)
        w_scale = sb("w_scale", [P, 1], F32, st2)

        tr_ps = ps("tr_ps", [P, 2, GW], F32, st2)
        acc_ps = ps("acc_ps", [P, 2, 2 * D], F32, st2)
        ep_ps = ps("ep_ps", [P, 512], F32, st2)
        lg_ps = ps("lg_ps", [P, 512], F32, st2)

        x_loaded = [sem(f"x_loaded{c}") for c in range(4)]
        adj_loaded = [sem(f"adj_loaded{a}") for a in range(RING)]
        res_loaded = [sem("res_loaded0"), sem("res_loaded1")]
        consts_loaded = sem("consts_loaded")
        ident_set = sem("ident_set")
        eps_set = sem("eps_set")
        constants_set = sem("constants_set")
        pool_waited = sem("pool_waited")
        ln_moments, ln_sdev, ln_scale, ln_scale_r, ln_chain = (
            sem("ln_moments"), sem("ln_sdev"), sem("ln_scale"), sem("ln_scale_r"), sem("ln_chain"))
        cur_f_ready, cur_hi_ready, cur_ready = sem("cur_f_ready"), sem("cur_hi_ready"), sem("cur_ready")
        mask_ready, count_ready, inc_ready = sem("mask_ready"), sem("count_ready"), sem("inc_ready")
        cnt_ready, root_ready, rclip_ready, rinv_ready = sem("cnt_ready"), sem("root_ready"), sem("rclip_ready"), sem("rinv_ready")
        transposed, hi_ready, lo_ready, multiplied = sem("transposed"), sem("hi_ready"), sem("lo_ready"), sem("multiplied")
        deg_ready, rdeg_ready, part_ready, part_x_ready = sem("deg_ready"), sem("rdeg_ready"), sem("part_ready"), sem("part_x_ready")
        x2_ready, x2_stats, x2_moments, sd_ready, rstd_ready, nmr_ready = (
            sem("x2_ready"), sem("x2_stats"), sem("x2_moments"), sem("sd_ready"), sem("rstd_ready"), sem("nmr_ready"))
        xn_ready, xhi_ready, xlo_ready, xnT_psum, xnT_ready = (
            sem("xn_ready"), sem("xhi_ready"), sem("xlo_ready"), sem("xnT_psum"), sem("xnT_ready"))
        logits_psum, logits_ready, top_ready, idx_ready = sem("logits_psum"), sem("logits_ready"), sem("top_ready"), sem("idx_ready")
        x2_stored = [sem("x2_stored0"), sem("x2_stored1")]
        xhl_stored = [sem("xhl_stored0"), sem("xhl_stored1")]

        w_loaded = [sem("w1_loaded"), sem("w2_loaded")]
        w_squared, w_summed, w_total, w_rooted, w_norm_ready, w_cut_ready, w_scale_ready = (
            sem("w_squared"), sem("w_summed"), sem("w_total"), sem("w_rooted"), sem("w_norm_ready"), sem("w_cut_ready"),
            sem("w_scale_ready"))
        w_scaled, w_hi_ready, w_parted, w_stored = sem("w_scaled"), sem("w_hi_ready"), sem("w_parted"), sem("w_stored")
        rows_stored = sem("rows_stored")

        st2.close()
        w_res = sb("w_resident", [P, E, 2, 2, W], F16)
        b2_all = sb("b2_all", [P, E, D], F32)
        ch = sb("relu_scale", [P, E], F32)
        c2 = sb("out_scale", [P, E], F32)
        b1s = sb("b1_scaled", [P, E, FC], F32)
        gather_idx = sb("gather_idx", [P, EXPERT_TILES, 2], U32)
        scatter_idx = sb("scatter_idx", [P, EXPERT_TILES, 2], U32)
        tile_expert = sb("tile_expert", [P, EXPERT_TILES], I32)

        st3 = ctx.enter_context(ExitStack())
        SLOTS = 2 * NT
        b1_rows = sb("b1_rows", [E * FC, P], F32, st3)
        b1_sq = sb("b1_sq", [P, E, FC], F32, st3)
        b1_sum = sb("b1_sum", [P, E], F32, st3)
        bound = sb("bound", [P, E], F32, st3)
        bound_c = sb("bound_c", [P, E], F32, st3)
        h_scale = sb("h_scale", [P, E], F32, st3)
        best = sb("best", [P, 2, NT], F32, st3)
        equal = sb("equal", [P, NT, E], F32, st3)
        ranked = sb("ranked", [P, NT, E], F32, st3)
        first = sb("first", [P, NT], F32, st3)
        rest = sb("rest", [P, NT, E], F32, st3)
        chosen = sb("chosen", [P, 2, NT, E], F32, st3)
        either = sb("either", [P, NT, E], BF16, st3)
        gap = sb("gap", [P, NT], F32, st3)
        gap_exp = sb("gap_exp", [P, NT], F32, st3)
        gate_den = sb("gate_den", [P, NT], F32, st3)
        gate = sb("gate", [P, 2, NT], F32, st3)
        gated = sb("gated", [P, 2, NT, E], F32, st3)
        comb = sb("comb", [P, NT, E], F32, st3)
        totals = sb("totals", [P, E, NT], F32, st3)
        running = sb("running", [P, E, NT], F32, st3)
        before = sb("before", [P, E, NT], F32, st3)
        n_tok = sb("n_tok", [P, E], F32, st3)
        n_pad = sb("n_pad", [P, E], I32, st3)
        n_tiles_i = sb("n_tiles_i", [P, E], I32, st3)
        n_tiles = sb("n_tiles", [P, E], F32, st3)
        tile_end = sb("tile_end", [P, E], F32, st3)
        tile_start = sb("tile_start", [P, E], F32, st3)
        offset = sb("offset", [P, E], F32, st3)
        place = sb("place", [P, E, NT], F32, st3)
        place2 = sb("place2", [P, E, NT], F32, st3)
        picked = sb("picked", [P, 2, NT, E], F32, st3)
        slot = sb("slot", [P, 2, NT], F32, st3)
        slot_i = sb("slot_i", [P, SLOTS], I32, st3)
        slot_hi_i = sb("slot_hi_i", [P, SLOTS], I32, st3)
        slot_lo_i = sb("slot_lo_i", [P, SLOTS], I32, st3)
        slot_hi = sb("slot_hi", [P, SLOTS], BF16, st3)
        slot_lo = sb("slot_lo", [P, SLOTS], BF16, st3)
        lane_hot = sb("lane_hot", [P, SLOTS, P], BF16, st3)
        half_hot = sb("half_hot", [P, 2, SLOTS // 4, HALVES], BF16, st3)
        half_val = sb("half_val", [P, SLOTS, 2, HALVES], BF16, st3)
        idx_a = sb("idx_a", [P, HALVES], F32, st3)
        idx_f = sb("idx_f", [P, EXPERT_TILES, 2], F32, st3)
        ended = sb("ended", [P, EXPERT_TILES, E], F32, st3)
        n_ended = sb("n_ended", [P, EXPERT_TILES], F32, st3)
        zero_rows = sb("zero_rows", [P, 2, D], F32, st3)
        rank_ps = ps("rank_ps", [P, 512], F32, st3)
        total_ps = ps("total_ps", [P, 512], F32, st3)
        b1_ps = ps("b1_ps", [P, 512], F32, st3)
        bn_ps = ps("bn_ps", [P, 512], F32, st3)
        idx_ps = ps("idx_ps", [P, 512], F32, st3)
        st3.close()

        x_g = sb("x_gathered", [P, 2, 2, XROW // 2], U32)
        g_idx = sb("g_idx", [P, 2, 2], U32)
        s_idx = sb("s_idx", [P, 2, 2], U32)
        x_t = sb("x_t", [P, 2, DC, TT], F16)
        tile_gate = sb("tile_gate", [P, 2, 2], F32)
        h_f = sb("h_f", [P, FC, TT], F32)
        h_hl = sb("h_hl", [P, 2, 2, FC, TT], F16)
        y1 = sb("y1", [P, 2, D], F32)
        y = sb("y", [P, 2, 2, D], F32)
        xt_ps = ps("xt_ps", [P, 2, DC, TT], F16)
        h_ps = ps("h_ps", [P, FC, TT], F32)
        y_ps = ps("y_ps", [P, 2, 2, D], F32)

        b1_loaded, b2_loaded, comb_stored, pads_cleared = sem("b1_loaded"), sem("b2_loaded"), sem("comb_stored"), sem("pads_cleared")
        b1_turned, b1_squared, b1_summed, b1_rooted = sem("b1_turned"), sem("b1_squared"), sem("b1_summed"), sem("b1_rooted")
        zeroed = sem("zeroed")
        route = sem("route")
        chosen_ready, ranks_ready, gap_ready, gap_exp_ready, comb_ready = (
            sem("chosen_ready"), sem("ranks_ready"), sem("gap_ready"), sem("gap_exp_ready"), sem("comb_ready"))
        hot_ready, half_ready, half_lo_ready, idx_summed, routed = (
            sem("hot_ready"), sem("half_ready"), sem("half_lo_ready"), sem("idx_summed"), sem("routed"))
        w_arrived = [sem("w_arrived0"), sem("w_arrived1")]
        w_resident = sem("w_resident_experts")
        idx_copied = sem("idx_copied")
        gathered = [sem("gathered0"), sem("gathered1")]
        x_turned, x_t_ready, gate_copied = sem("x_turned"), sem("x_t_ready"), sem("gate_copied")
        product1, relu_ready, h_hi_ready, h_lo_ready = sem("product1"), sem("relu_ready"), sem("h_hi_ready"), sem("h_lo_ready")
        product2, y1_ready, y_ready = sem("product2"), sem("y1_ready"), sem("y_ready")
        s_idx_copied, scattered = sem("s_idx_copied"), sem("scattered")

        def spread(ap, shape):
            return ap.broadcast_to(shape)

        def experts_looped(eng, step):
            for s in range(3):
                step(s, s % 2)
            with eng.Fori(0, (EXPERT_TILES - 3) // 2) as i:
                step(i * 2 + 3, 1)
                step(i * 2 + 4, 0)

        def resident_weights(sp):
            sp.wait_ge(logits_ready, NT)
            sp.wait_ge(rows_stored, 1)
            sp.dma_start(b1_rows[:], b1.rearrange("e (c p) -> (e c) p", p=P)).then_inc(b1_loaded, 16)
            sp.dma_start(w_res[:, 0, :, :, :].rearrange("p m h w -> p m (h w)"), w_hl[0].rearrange("m p h w -> p m (h w)")
                         ).then_inc(w_arrived[0], 16)
            sp.wait_ge(zeroed, 1)
            sp.dma_start(out[N:PADS, :].rearrange("(h p) d -> p h d", p=P), zero_rows[:]).then_inc(pads_cleared, 16)
            sp.dma_start(b2_all[:].rearrange("p e d -> p (e d)"),
                         b2.rearrange("(o e) d -> o (e d)", o=1).broadcast_to([P, E * D])).then_inc(b2_loaded, 16)
            sp.wait_ge(comb_ready, 1)
            sp.dma_start(xtab[:, D:D + E].rearrange("(t p) e -> p t e", p=P), comb[:].bitcast(U32)
                         ).then_inc(comb_stored, 16)
            for e in range(1, E):
                sp.dma_start(w_res[:, e, :, :, :].rearrange("p m h w -> p m (h w)"), w_hl[e].rearrange("m p h w -> p m (h w)")
                             ).then_inc(w_arrived[e % 2], 16)
                sp.wait_ge(w_arrived[(e - 1) % 2], 16 * ((e - 1) // 2 + 1))
                sp.sem_inc(w_resident, 1)
            sp.wait_ge(w_arrived[(E - 1) % 2], 16 * ((E - 1) // 2 + 1))
            sp.sem_inc(w_resident, 1)
            sp.wait_ge(comb_stored, 16)
            sp.wait_ge(pads_cleared, 16)

        def dve_routing(dve):
            steps = [0]

            def link(ins):
                steps[0] += 1
                ins.then_inc(route, 1)
                dve.wait_ge(route, steps[0])

            TE = [P, NT, E]
            V = nc.vector
            dve.wait_ge(rows_stored, 1)
            dve.wait_ge(logits_ready, NT)
            dve.wait_ge(constants_set, 11)
            V.memset(zero_rows[:], 0.0).then_inc(zeroed, 1)
            for k in range(2):
                src = logits if k == 0 else rest
                link(V.tensor_reduce(best[:, k, :], src[:], AX_X, ALU.max))
                link(V.tensor_tensor(equal[:], src[:], spread(best[:, k, :].rearrange("p (t o) -> p t o", o=1), TE), ALU.is_equal))
                link(V.tensor_tensor(ranked[:], equal[:], spread(order_e[:].rearrange("p (o e) -> p o e", o=1), TE), ALU.mult))
                link(V.tensor_reduce(first[:], ranked[:], AX_X, ALU.max))
                link(V.tensor_tensor(chosen[:, k, :, :], ranked[:], spread(first[:].rearrange("p (t o) -> p t o", o=1), TE), ALU.is_equal))
                if k == 0:
                    link(V.scalar_tensor_tensor(rest[:], chosen[:, 0, :, :], -3.0e38, logits[:], ALU.mult, ALU.add))
            V.tensor_tensor(either[:], chosen[:, 0, :, :], chosen[:, 1, :, :], ALU.add).then_inc(chosen_ready, 1)
            V.tensor_tensor(gap[:], best[:, 1, :], best[:, 0, :], ALU.subtract).then_inc(gap_ready, 1)
            dve.wait_ge(ranks_ready, 1)
            link(V.tensor_copy(totals[:], total_ps[:, 0:NT * E].rearrange("p (t e) -> p e t", e=E)))
            flat = lambda a: a[:].rearrange("p e t -> p (e t)")
            link(V.tensor_tensor_scan(flat(running), ones_row[:, 0:NT * E], flat(totals), 0.0, ALU.mult, ALU.add))
            link(V.tensor_tensor(before[:], running[:], totals[:], ALU.subtract))
            link(V.tensor_tensor(n_tok[:], running[:, :, NT - 1], before[:, :, 0], ALU.subtract))
            link(V.tensor_scalar(n_pad[:], n_tok[:], float(TT - 1), None, ALU.add))
            link(V.tensor_scalar(n_tiles_i[:], n_pad[:], 8, None, ALU.arith_shift_right))
            link(V.tensor_copy(n_tiles[:], n_tiles_i[:]))
            link(V.tensor_tensor_scan(tile_end[:], ones_row[:, 0:E], n_tiles[:], 0.0, ALU.mult, ALU.add))
            link(V.tensor_tensor(tile_start[:], tile_end[:], n_tiles[:], ALU.subtract))
            link(V.scalar_tensor_tensor(offset[:], tile_start[:], float(TT), before[:, :, 0], ALU.mult, ALU.subtract))
            link(V.tensor_tensor(place[:], rank_ps[:, 0:NT * E].rearrange("p (t e) -> p e t", e=E), before[:], ALU.add))
            link(V.tensor_tensor(place2[:], place[:], spread(offset[:].rearrange("p (e o) -> p e o", o=1), [P, E, NT]), ALU.add))
            for k in range(2):
                link(V.tensor_tensor(picked[:, k, :, :], place2[:].rearrange("p e t -> p t e"), chosen[:, k, :, :], ALU.mult))
                link(V.tensor_reduce(slot[:, k, :], picked[:, k, :, :], AX_X, ALU.add))
            link(V.tensor_copy(slot_i[:], slot[:].rearrange("p k t -> p (k t)")))
            link(V.tensor_scalar(slot_lo_i[:], slot_i[:], P - 1, None, ALU.bitwise_and))
            link(V.tensor_scalar(slot_hi_i[:], slot_i[:], 7, None, ALU.arith_shift_right))
            link(V.tensor_copy(slot_lo[:], slot_lo_i[:]))
            link(V.tensor_copy(slot_hi[:], slot_hi_i[:]))
            for q in range(4):
                j = slice(q * SLOTS // 4, (q + 1) * SLOTS // 4)
                n = SLOTS // 4
                if q >= 2:
                    dve.wait_ge(half_lo_ready, q - 1)
                    dve.wait_ge(hot_ready, q - 1)
                V.tensor_tensor(half_hot[:, q % 2, :, :], spread(lanes_b[:, 0:HALVES].rearrange("p (o h) -> p o h", o=1), [P, n, HALVES]),
                                spread(slot_hi[:, j].rearrange("p (j o) -> p j o", o=1), [P, n, HALVES]), ALU.is_equal
                                ).then_inc(half_ready, 1)
                V.tensor_tensor(lane_hot[:, j, :], spread(lanes_b[:].rearrange("p (o h) -> p o h", o=1), [P, n, P]),
                                spread(slot_lo[:, j].rearrange("p (j o) -> p j o", o=1), [P, n, P]), ALU.is_equal)
                dve.wait_ge(half_ready, q + 1)
                V.tensor_tensor(half_val[:, j, 0, :], half_hot[:, q % 2, :, :],
                                spread(tok_hi[:, j].rearrange("p (j o) -> p j o", o=1), [P, n, HALVES]), ALU.mult
                                ).then_inc(hot_ready, 1)
            dve.wait_ge(gap_exp_ready, 1)
            link(V.tensor_scalar(gate_den[:], gap_exp[:], 1.0, None, ALU.add))
            link(V.reciprocal(gate[:, 0, :], gate_den[:]))
            link(V.tensor_tensor(gate[:, 1, :], gate[:, 0, :], gap_exp[:], ALU.mult))
            link(V.tensor_tensor(gated[:], chosen[:], spread(gate[:].rearrange("p k (t o) -> p k t o", o=1), [P, 2, NT, E]), ALU.mult))
            V.tensor_tensor(comb[:], gated[:, 0, :, :], gated[:, 1, :, :], ALU.add).then_inc(comb_ready, 1)
            link(V.tensor_tensor(ended[:], spread(tile_end[:].rearrange("p (o e) -> p o e", o=1), [P, EXPERT_TILES, E]),
                                 spread(lanes[:, 0:EXPERT_TILES].rearrange("p (j o) -> p j o", o=1), [P, EXPERT_TILES, E]), ALU.is_le))
            link(V.tensor_reduce(n_ended[:], ended[:], AX_X, ALU.add))
            link(V.tensor_scalar(tile_expert[:], n_ended[:], float(E - 1), None, ALU.min))
            dve.wait_ge(b1_turned, 1)
            link(V.tensor_copy(b1t[:], b1_ps[:, 0:E * FC].rearrange("p (e c) -> p e c", c=FC)))
            link(V.tensor_tensor(b1_sq[:], b1t[:], b1t[:], ALU.mult))
            V.tensor_reduce(b1_sum[:], b1_sq[:], AX_X, ALU.add).then_inc(b1_squared, 1)
            dve.wait_ge(b1_rooted, 1)
            link(V.scalar_tensor_tensor(bound[:], w_norm[:, 0, :], float(D) ** 0.5, b_norm[:], ALU.mult, ALU.add))
            link(V.tensor_scalar(bound_c[:], bound[:], TINY, 1.0 / H_TOP, ALU.max, ALU.mult))
            link(V.reciprocal(h_scale[:], bound_c[:]))
            link(V.scalar_tensor_tensor(ch[:], h_scale[:], 1.0 / (X_SCALE * W_TOP), w_norm[:, 0, :], ALU.mult, ALU.mult))
            link(V.tensor_tensor(b1s[:], b1t[:], spread(h_scale[:].rearrange("p (e o) -> p e o", o=1), [P, E, FC]), ALU.mult))
            link(V.scalar_tensor_tensor(c2[:], bound_c[:], 1.0 / W_TOP, w_norm[:, 1, :], ALU.mult, ALU.mult))
            dve.wait_ge(idx_summed, 1)
            link(V.tensor_scalar(idx_a[:], idx_ps[:, 0:HALVES], -float(P), 2.0 * N, ALU.mult, ALU.add))
            link(V.tensor_tensor(idx_f[:].rearrange("p j h -> p (j h)"), idx_a[:], idx_ps[:, HALVES:2 * HALVES], ALU.add))
            link(V.tensor_scalar(gather_idx[:], idx_f[:], float(N - 1), None, ALU.min))
            link(V.tensor_tensor(scatter_idx[:], idx_f[:], spread(pad_rows[:].rearrange("p (o h) -> p o h", o=1), [P, EXPERT_TILES, 2]), ALU.min))
            dve.sem_inc(routed, 1)

        def pe_routing(pe):
            pe.wait_ge(b1_loaded, 16)
            nc.tensor.transpose(b1_ps[:, 0:E * FC], b1_rows[:], ident[0:E * FC, 0:E * FC]).then_inc(b1_turned, 1)
            pe.wait_ge(chosen_ready, 1)
            sel = either[:].rearrange("p t e -> p (t e)")
            nc.tensor.matmul(rank_ps[:, 0:NT * E], earlier[:], sel, start=True, stop=True)
            nc.tensor.matmul(total_ps[:, 0:NT * E], ones_b[:], sel, start=True, stop=True).then_inc(ranks_ready, 1)
            for q in range(4):
                pe.wait_ge(hot_ready, q + 1)
                pe.wait_ge(half_lo_ready, q + 1)
                for j in range(q * SLOTS // 4, (q + 1) * SLOTS // 4):
                    m = nc.tensor.matmul(idx_ps[:, 0:2 * HALVES], lane_hot[:, j, :],
                                         half_val[:, j, :, :].rearrange("p v h -> p (v h)"), start=(j == 0), stop=(j == SLOTS - 1))
            m.then_inc(idx_summed, 1)
            pe.wait_ge(b1_squared, 1)
            nc.tensor.matmul(bn_ps[:, 0:E], ones_f[:], b1_sum[:], start=True, stop=True).then_inc(b1_summed, 1)

        def act_routing(act):
            act.wait_ge(gap_ready, 1)
            nc.scalar.activation(gap_exp[:], gap[:], ACT.Exp).then_inc(gap_exp_ready, 1)
            for q in range(4):
                act.wait_ge(half_ready, q + 1)
                j = slice(q * SLOTS // 4, (q + 1) * SLOTS // 4)
                nc.scalar.activation(half_val[:, j, 1, :], half_hot[:, q % 2, :, :], ACT.Copy, scale=lane_col[:, 0:1]
                                     ).then_inc(half_lo_ready, 1)
            act.wait_ge(b1_summed, 1)
            nc.scalar.activation(b_norm[:], bn_ps[:, 0:E], ACT.Sqrt).then_inc(b1_rooted, 1)

        def tile_e(eng, s):
            return eng.value_load(tile_expert[0:1, bass.ds(s, 1)], min_val=0, max_val=E - 1)

        def pe_experts(pe):
            pe.wait_ge(routed, 1)

            def turn(s, u):
                wait(pe, gathered[u], (s // 2 + 1) * 32 if is_static(s) else (s - u) * 16 + 32)
                wait(pe, x_t_ready, s)
                for hl in range(2):
                    for c in range(DC):
                        for half in range(2):
                            m = nc.tensor.transpose(xt_ps[:, hl, c, half * P:(half + 1) * P],
                                                    x_g[:, u, half, :].bitcast(F16)[:, hl * D + c * P:hl * D + (c + 1) * P], ident16[:])
                m.then_inc(x_turned, 1)

            def first_product(s, u):
                e = tile_e(pe, s)
                pe.wait_ge(w_resident, e + 1)
                pe.wait_ge(x_t_ready, s + 1)
                for f in range(FC):
                    if f % 2 == 0:
                        wait(pe, relu_ready, (s - 1) * FC + f + 2)
                    o = h_ps[:, f, :]
                    n = 0
                    for wh, xh in ((0, 0), (0, 1), (1, 0)):
                        for c in range(DC):
                            m = nc.tensor.matmul(o, w_res[:, bass.ds(e, 1), 0, wh, c * F + f * P:c * F + (f + 1) * P
                                                          ].rearrange("p o f -> p (o f)"),
                                                 x_t[:, xh, c, :], start=(n == 0), stop=(n == 3 * DC - 1))
                            n += 1
                    if f % 2 == 1:
                        m.then_inc(product1, 1)

            def second_product(s, u):
                e = tile_e(pe, s)
                pe.wait_ge(h_lo_ready, s * 2 + 2)
                wait(pe, y1_ready, s - 1)
                for half in range(2):
                    n = 0
                    for f in range(FC):
                        for hh, wh in ((0, 0), (1, 0), (0, 1)):
                            m = nc.tensor.matmul(y_ps[:, u, half, :], h_hl[:, u, hh, f, half * P:(half + 1) * P],
                                                 w_res[:, bass.ds(e, 1), 1, wh, f * D:(f + 1) * D].rearrange("p o d -> p (o d)"),
                                                 start=(n == 0), stop=(n == 3 * FC - 1))
                            n += 1
                m.then_inc(product2, 1)

            def step(s, u):
                turn(s, u)
                if not is_static(s) or s >= 2:
                    second_product(s - 2, u)
                first_product(s, u)

            experts_looped(pe, step)
            second_product(EXPERT_TILES - 2, (EXPERT_TILES - 2) % 2)
            second_product(EXPERT_TILES - 1, (EXPERT_TILES - 1) % 2)

        def act_experts(act):
            act_routing(act)
            act.wait_ge(routed, 1)

            def step(s, u):
                e = tile_e(act, s)
                for f in range(FC):
                    if f % 2 == 0:
                        act.wait_ge(product1, s * (FC // 2) + f // 2 + 1)
                    if f % (FC // 2) == 0:
                        wait(act, h_lo_ready, (s - 1) * 2 + f // (FC // 2) + 1)
                    nc.scalar.activation(h_f[:, f, :], h_ps[:, f, :], ACT.Relu, bias=b1s[:, bass.ds(e, 1), f],
                                         scale=ch[:, bass.ds(e, 1)]).then_inc(relu_ready, 1)
                    if f % (FC // 2) == FC // 2 - 1:
                        act.wait_ge(relu_ready, s * FC + f + 1)
                        if f < FC // 2:
                            wait(act, product2, s - 1)
                        fs = slice(f + 1 - FC // 2, f + 1)
                        nc.scalar.activation(h_hl[:, u, 0, fs, :], h_f[:, fs, :], ACT.Copy).then_inc(h_hi_ready, 1)

            experts_looped(act, step)

        def dve_experts(dve):
            dve.wait_ge(routed, 1)
            dve.wait_ge(b2_loaded, 16)

            def combine(s, u):
                e = tile_e(dve, s)
                dve.wait_ge(product2, s + 1)
                wait(dve, y_ready, s)
                nc.vector.scalar_tensor_tensor(y1[:], y_ps[:, u, :, :], c2[:, bass.ds(e, 1)],
                                               spread(b2_all[:, bass.ds(e, 1), :], [P, 2, D]), ALU.mult, ALU.add
                                               ).then_inc(y1_ready, 1)
                dve.wait_ge(y1_ready, s + 1)
                wait(dve, scattered, (s - 1) * 32)
                for half in range(2):
                    m = nc.vector.tensor_scalar(y[:, u, half, :], y1[:, half, :], tile_gate[:, u, half:half + 1], None, ALU.mult)
                m.then_inc(y_ready, 1)

            def step(s, u):
                dve.wait_ge(x_turned, s + 1)
                flat4 = lambda a: a.rearrange("p h c t -> p (h c t)")
                nc.vector.tensor_copy(flat4(x_t[:]), flat4(xt_ps[:])).then_inc(x_t_ready, 1)
                if not is_static(s) or s >= 2:
                    combine(s - 2, u)
                e = tile_e(dve, s)
                wait(dve, y_ready, s - 1)
                nc.vector.tensor_copy(tile_gate[:, u, :].rearrange("p (h o) -> p h o", o=1),
                                      x_g[:, u, :, :].bitcast(F32)[:, :, bass.ds(e + D, 1)]).then_inc(gate_copied, 1)
                for h in range(2):
                    dve.wait_ge(h_hi_ready, s * 2 + h + 1)
                    fs = slice(h * FC // 2, (h + 1) * FC // 2)
                    nc.vector.tensor_tensor(h_hl[:, u, 1, fs, :], h_f[:, fs, :], h_hl[:, u, 0, fs, :], ALU.subtract
                                            ).then_inc(h_lo_ready, 1)

            experts_looped(dve, step)
            combine(EXPERT_TILES - 2, (EXPERT_TILES - 2) % 2)
            combine(EXPERT_TILES - 1, (EXPERT_TILES - 1) % 2)

        def pool_experts(pool):
            pool.wait_ge(routed, 1)
            pool.wait_ge(comb_stored, 16)
            pool.wait_ge(pads_cleared, 16)

            def gather(s, u):
                wait_apart(pool, gate_copied, s - 1)
                wait_apart(pool, x_turned, s - 1)
                nc.gpsimd.tensor_copy(g_idx[:, u, :], gather_idx[:, bass.ds(s, 1), :].rearrange("p o h -> p (o h)")
                                      ).then_inc(idx_copied, 1)
                wait_apart(pool, idx_copied, s + 1)
                for half in range(2):
                    nc.gpsimd.indirect_dma_start(x_g[:, u, half, :], None, xtab[:, :],
                                                 bass.IndirectOffsetOnAxis(ap=g_idx[:, u, half:half + 1], axis=0)
                                                 ).then_inc(gathered[u], 16)

            def scatter(s, u):
                wait_apart(pool, scattered, s * 32)
                nc.gpsimd.tensor_copy(s_idx[:, u, :], scatter_idx[:, bass.ds(s, 1), :].rearrange("p o h -> p (o h)")
                                      ).then_inc(s_idx_copied, 1)
                wait_apart(pool, s_idx_copied, s + 1)
                wait_apart(pool, y_ready, s + 1)
                for half in range(2):
                    nc.gpsimd.indirect_dma_start(out[:, :], bass.IndirectOffsetOnAxis(ap=s_idx[:, u, half:half + 1], axis=0),
                                                 y[:, u, half, :], None, compute_op=ALU.add).then_inc(scattered, 16)

            def step(s, u):
                gather(s, u)
                if not is_static(s) or s >= 3:
                    scatter(s - 3, (u + 1) % 2)

            experts_looped(pool, step)
            for s in range(EXPERT_TILES - 3, EXPERT_TILES):
                scatter(s, s % 2)
            pool.wait_ge(scattered, EXPERT_TILES * 32)

        block = ctx.enter_context(nc.Block())

        def tiles_looped(eng, step, first, last):
            for i in range(first):
                for u in range(4):
                    step(4 * i + u, u, i)
            with eng.Fori(first, NT // 4 - last) as i:
                for u in range(4):
                    step(i * 4 + u, u, i)
            for i in range(NT // 4 - last, NT // 4):
                for u in range(4):
                    step(4 * i + u, u, i)

        @block.sync
        def _(sp):
            def load_x(c):
                if c >= 4:
                    sp.wait_ge(cur_f_ready, XCH * (c - 3))
                sp.dma_start(x_in[:, c % 4, :, :], x[c * XCH * P:(c + 1) * XCH * P, :].rearrange("(t p) d -> p t d", p=P)
                             ).then_inc(x_loaded[c % 4], 16)

            def load_adj(t, u):
                wait(sp, transposed, GROUPS * (t - RING) + GROUPS)
                sp.dma_start(adj_t[:, u, :], adj[bass.ds(t * P, P), :]).then_inc(adj_loaded[u], 16)

            def load_res(t, u):
                wait(sp, part_x_ready, t - 1)
                sp.dma_start(x_res[:, u % 2, :], x[bass.ds(t * P, P), :]).then_inc(res_loaded[u % 2], 16)

            def load_weights(e, which):
                n = e * 2 + which
                if is_static(n) and n == 0:
                    sp.wait_ge(cur_ready, NT // XCH)
                wait(sp, w_parted, (n - 2) * 2 + 2)
                src = (w1[bass.ds(e, 1), :, :].rearrange("o (c p) f -> p (o c) f", p=P) if which == 0 else
                       w2[bass.ds(e, 1), :, :].rearrange("o (c p) d -> p (o c) d", p=P))
                sp.dma_start(w_in[:, which, :].rearrange("p (c f) -> p c f", c=DC if which == 0 else FC), src
                             ).then_inc(w_loaded[which], 16)

            def store_weights(e, which):
                sp.wait_ge(w_parted, (e * 2 + which) * 2 + 2)
                sp.dma_start(w_hl[bass.ds(e, 1), which, :, :, :].rearrange("o p h w -> p (o h) w"), w_parts[:]
                             ).then_inc(w_stored, 16)

            def step(t, u, i):
                if not is_static(t) or t + 3 < NT:
                    load_adj(t + 3, (u + 3) % 4)
                load_res(t, u)
                if u == 0:
                    load_weights(i, 0)
                    if not is_static(i) or i >= 1:
                        store_weights(i - 1, 0)
                if u == 2:
                    load_weights(i, 1)
                    if not is_static(i) or i >= 1:
                        store_weights(i - 1, 1)

            for c in range(4):
                load_x(c)
            load_adj(0, 0)
            for c in range(4, NT // XCH):
                load_x(c)
            load_adj(1, 1)
            load_adj(2, 2)
            tiles_looped(sp, step, 1, 1)
            store_weights(E - 1, 0)
            store_weights(E - 1, 1)
            sp.wait_ge(w_stored, 16 * 2 * E)
            resident_weights(sp)

        def wait_apart(pool, semaphore, value):
            if is_static(value) and value <= 0:
                return
            pool.wait_ge(semaphore, value)
            pool.sem_inc(pool_waited, 1)

        @block.gpsimd
        def _(pool):
            nc.gpsimd.memset(ident[:], 0.0).then_inc(ident_set, 1)
            pool.wait_ge(ident_set, 1)
            nc.gpsimd.affine_select(out=ident[:], in_=ident[:], compare_op=ALU.not_equal, fill=1.0, base=0,
                                    pattern=[[-1, P]], channel_multiplier=1).then_inc(ident_set, 1)

            def numbers(a, pattern, base, across):
                nc.gpsimd.iota(a, pattern, base=base, channel_multiplier=across, allow_small_or_imprecise_dtypes=True
                               ).then_inc(constants_set, 1)

            pool.wait_ge(ident_set, 2)
            nc.gpsimd.tensor_copy(ident16[:], ident[:]).then_inc(constants_set, 1)
            numbers(lanes[:], [[1, P]], 0, 0)
            numbers(lanes_b[:], [[1, P]], 0, 0)
            numbers(lane_col[:], [[0, 1]], 0, 1)
            numbers(order_e[:], [[-1, E]], E, 0)
            numbers(tok_hi[:], [[0, 2], [-1, NT]], 2 * N // P, 0)
            numbers(pad_rows[:], [[P, 2]], N, 1)
            nc.gpsimd.memset(ones_b[:], 1.0).then_inc(constants_set, 1)
            nc.gpsimd.memset(ones_f[:], 1.0).then_inc(constants_set, 1)
            nc.gpsimd.memset(ones_row[:], 1.0).then_inc(constants_set, 1)
            pool.wait_ge(constants_set, 10)
            nc.gpsimd.affine_select(out=earlier[:], in_=ones_b[:], compare_op=ALU.is_gt, fill=0.0, base=0,
                                    pattern=[[1, P]], channel_multiplier=-1).then_inc(constants_set, 1)

            for c in range(NT // XCH):
                pool.wait_ge(cur_hi_ready, c + 1)
                nc.gpsimd.tensor_tensor(cur[:, c * XCH:(c + 1) * XCH, 1, :], cur_f[:, c % 2, :, :],
                                        cur32[:, c * XCH:(c + 1) * XCH, 0, :], ALU.subtract).then_inc(cur_ready, 1)

            def sum_squares(e, which):
                n = e * 2 + which
                pool.wait_ge(w_squared, n * 2 + 2)
                nc.gpsimd.tensor_tensor(w_sum[:], w_sq[:, 0:1], w_sq[:, 1:2], ALU.add).then_inc(w_summed, 1)
                wait_apart(pool, w_summed, n + 1)
                nc.gpsimd.partition_all_reduce(w_tot[:], w_sum[:], P, RADD).then_inc(w_total, 1)

            def split_weights(e, which):
                n = e * 2 + which
                wait(pool, w_stored, n * 16)
                for h in range(2):
                    cols = slice(h * WH, (h + 1) * WH)
                    wait_apart(pool, w_scaled, n * 2 + h + 1)
                    nc.gpsimd.tensor_copy(w_parts[:, 0, cols], w_in[:, which, cols]).then_inc(w_hi_ready, 1)
                    pool.wait_ge(w_hi_ready, n * 2 + h + 1)
                    nc.gpsimd.tensor_tensor(w_parts[:, 1, cols], w_in[:, which, cols], w_parts[:, 0, cols], ALU.subtract
                                            ).then_inc(w_parted, 1)

            def epilogue(t, u):
                pool.wait_ge(part_ready, t + 1)
                wait(pool, res_loaded[u % 2], (t // 2 + 1) * 16 if is_static(t) else ((t - u % 2) * 8 + 16))
                nc.gpsimd.tensor_tensor(part[:, u % 2, :], part[:, u % 2, :], x_res[:, u % 2, :], ALU.add
                                        ).then_inc(part_x_ready, 1)

            def low(t, u):
                pool.wait_ge(xhi_ready, t + 1)
                nc.gpsimd.tensor_tensor(xhl[:, u % 2, 1, :], xn[:, u % 2, :], xhl[:, u % 2, 0, :], ALU.subtract
                                        ).then_inc(xlo_ready, 1)

            def step(t, u, i):
                epilogue(t, u)
                if not is_static(t) or t >= 1:
                    low(t - 1, u - 1)

                if u == 2:
                    split_weights(i, 0)
                if u == 0 and (not is_static(i) or i >= 1):
                    split_weights(i - 1, 1)
                if u == 1:
                    sum_squares(i, 0)
                if u == 3:
                    sum_squares(i, 1)

            tiles_looped(pool, step, 1, 1)
            split_weights(E - 1, 1)
            low(NT - 1, 3)
            pool_experts(pool)

        @block.scalar
        def _(act):
            act.dma_start(rw[:], router_w.rearrange("(c p) e -> p c e", p=P)).then_inc(consts_loaded, 16)
            act.dma_start(rb[:], router_b.rearrange("(o e) -> o e", o=1).broadcast_to([P, E])).then_inc(consts_loaded, 16)
            act.wait_ge(eps_set, 1)
            def ln_root(c):
                act.wait_ge(ln_moments, XCH * (c + 1))
                nc.scalar.activation(sdev[:, c % 2, :], mom[:, c % 2, :, 1], ACT.Sqrt, bias=eps_c[:, 0:1]
                                     ).then_inc(ln_sdev, 1)

            def ln_apply(c):
                act.wait_ge(ln_scale, c + 1)
                if c >= 2:
                    act.wait_ge(cur_ready, c - 1)
                for k in range(XCH):
                    nc.scalar.activation(cur_f[:, c % 2, k, :], x_in[:, c % 4, k, :], ACT.Identity,
                                         bias=nmr[:, c % 2, k:k + 1], scale=rstd[:, c % 2, k:k + 1]).then_inc(cur_f_ready, 1)
                act.wait_ge(cur_f_ready, XCH * (c + 1))
                nc.scalar.activation(cur[:, c * XCH:(c + 1) * XCH, 0, :], cur_f[:, c % 2, :, :], ACT.Copy
                                     ).then_inc(cur_hi_ready, 1)

            for c in range(NT // XCH):
                ln_root(c)
                if c >= 1:
                    ln_apply(c - 1)
            ln_apply(NT // XCH - 1)

            def count(t, u, g):
                act.wait_ge(mask_ready, t * GROUPS + g + 1)
                m = mask[:, u % 2, g * GW:(g + 1) * GW]
                nc.scalar.activation(m, m, ACT.Copy, accum_out=cnt4[:, u % 2, g:g + 1]).then_inc(count_ready, 1)

            def sqrt_count(t, u):
                act.wait_ge(cnt_ready, t + 1)
                nc.scalar.activation(root[:, u % 2:u % 2 + 1], cnt[:, u % 2:u % 2 + 1], ACT.Sqrt).then_inc(root_ready, 1)

            def split_hi(t, u, g):
                act.wait_ge(transposed, t * GROUPS + g + 1)
                wait(act, multiplied, t * GROUPS + g - 1)
                nc.scalar.activation(inc_hi[:, g % 2, :], tr_ps[:, g % 2, :], ACT.Copy).then_inc(hi_ready, 1)

            def add_half(t, u):
                b = u % 2
                act.wait_ge(multiplied, (t + 1) * GROUPS)
                act.wait_ge(rdeg_ready, t + 1)
                nc.scalar.activation(part[:, b, :], acc_ps[:, b, D:2 * D], ACT.Copy, scale=rdeg[:, b:b + 1]
                                     ).then_inc(part_ready, 1)

            def root_variance(t, u):
                act.wait_ge(x2_moments, t + 1)
                nc.scalar.activation(sd_b[:], mom_b[:, 1:2], ACT.Sqrt, bias=eps_c[:, 0:1]).then_inc(sd_ready, 1)

            def normalise(t, u):
                b = u % 2
                act.wait_ge(nmr_ready, t + 1)
                wait(act, xlo_ready, t - 1)
                nc.scalar.activation(xn[:, b, :], x2[:, b, :], ACT.Identity, bias=nmr_b[:, 0:1], scale=rstd_b[:, 0:1]
                                     ).then_inc(xn_ready, 1)
                act.wait_ge(xn_ready, t + 1)
                if not is_static(t) or t >= 2:
                    wait(act, xhl_stored[b], (t - b) * 8)
                nc.scalar.activation(xhl[:, b, 0, :], xn[:, b, :], ACT.Copy).then_inc(xhi_ready, 1)

            def copy_transposed(t):
                act.wait_ge(xnT_psum, t + 1)
                nc.scalar.activation(xnT[:].rearrange("p c t -> p (c t)"), ep_ps[:, 0:D], ACT.Copy
                                     ).then_inc(xnT_ready, 1)

            def store(t, u):
                b = u % 2
                act.wait_ge(x2_ready, t + 1)
                act.dma_start(out[bass.ds(t * P, P), :], x2[:, b, :]).then_inc(x2_stored[b], 16)

            def store_input(t, u):
                b = u % 2
                act.wait_ge(xlo_ready, t + 1)
                act.dma_start(xtab[bass.ds(t * P, P), 0:D], xhl[:, b, :, :].rearrange("p h d -> p (h d)").bitcast(U32)
                              ).then_inc(xhl_stored[b], 16)

            def square_weights(e, which, h):
                n = e * 2 + which
                if h == 0:
                    act.wait_ge(w_loaded[which], e * 16 + 16)
                    wait(act, w_total, n)
                wait(act, w_squared, n * 2 + h)
                nc.scalar.activation(w_junk[:], w_in[:, which, h * WH:(h + 1) * WH], ACT.Square,
                                     accum_out=w_sq[:, h:h + 1]).then_inc(w_squared, 1)

            def root_weights(e, which):
                act.wait_ge(w_total, e * 2 + which + 1)
                nc.scalar.activation(w_root[:], w_tot[:], ACT.Sqrt).then_inc(w_rooted, 1)

            def scale_weights(e, which, h):
                if h == 0:
                    act.wait_ge(w_scale_ready, e * 2 + which + 1)
                cols = w_in[:, which, h * WH:(h + 1) * WH]
                nc.scalar.activation(cols, cols, ACT.Copy, scale=w_scale[:, 0:1]).then_inc(w_scaled, 1)

            def weights(u, i, g):
                if u % 2 == 1 and g % 2 == 1:
                    square_weights(i, u // 2, g // 2)
                if u % 2 == 0 and (u == 2 or not is_static(i) or i >= 1):
                    e = i if u == 2 else i - 1
                    if g == 0:
                        root_weights(e, (u // 2 + 1) % 2)
                    if g % 2 == 1:
                        scale_weights(e, (u // 2 + 1) % 2, g // 2)

            for g in range(GROUPS):
                count(0, 0, g)
            sqrt_count(0, 0)
            for g in range(GROUPS - 1):
                count(1, 1, g)

            def step(t, u, i):
                behind = lambda k: not is_static(t) or t >= k
                ahead = lambda k: not is_static(t) or t + k < NT
                for g in range(GROUPS):
                    split_hi(t, u, g)
                    if g == 0 and behind(1):
                        add_half(t - 1, u - 1)
                    if g == 0 and ahead(1):
                        count(t + 1, u + 1, GROUPS - 1)
                    if g >= 1 and ahead(2):
                        count(t + 2, u, g - 1)
                    if g == 0 and behind(2):
                        normalise(t - 2, u - 2)
                    if g == 2 and ahead(1):
                        sqrt_count(t + 1, u + 1)
                    if g == 2 and behind(1):
                        store(t - 1, u - 1)
                    if g == 2 and behind(2):
                        copy_transposed(t - 2)
                        store_input(t - 2, u - 2)
                    if g == 3 and behind(1):
                        root_variance(t - 1, u - 1)
                    weights(u, i, g)

            tiles_looped(act, step, 1, 1)
            add_half(NT - 1, 3)
            normalise(NT - 2, 2)
            for g in range(GROUPS):
                weights(0, NT // 4, g)
            store(NT - 1, 3)
            copy_transposed(NT - 2)
            store_input(NT - 2, 2)
            root_variance(NT - 1, 3)
            normalise(NT - 1, 3)
            copy_transposed(NT - 1)
            store_input(NT - 1, 3)
            for b in range(2):
                act.wait_ge(x2_stored[b], 16 * (NT // 2))
                act.wait_ge(xhl_stored[b], 16 * (NT // 2))
            act.sem_inc(rows_stored, 1)
            act_experts(act)

        @block.vector
        def _(dve):
            nc.vector.memset(eps_c[:], LN_EPS).then_inc(eps_set, 1)
            for c in range(NT // XCH):
                dve.wait_ge(x_loaded[c % 4], 16 * (c // 4 + 1))
                for k in range(XCH):
                    nc.vector.bn_stats(stats[:, k, :], x_in[:, c % 4, k, :]).then_inc(ln_chain, 1)
                dve.wait_ge(ln_chain, XCH * (c + 1))
                for k in range(XCH):
                    nc.vector.bn_aggr(mom[:, c % 2, k, :], stats[:, k, :]).then_inc(ln_moments, 1)
                dve.wait_ge(ln_sdev, c + 1)
                if c >= 2:
                    dve.wait_ge(cur_f_ready, XCH * (c - 1))
                nc.vector.reciprocal(rstd[:, c % 2, :], sdev[:, c % 2, :]).then_inc(ln_scale_r, 1)
                dve.wait_ge(ln_scale_r, c + 1)
                nc.vector.scalar_tensor_tensor(nmr[:, c % 2, :], mom[:, c % 2, :, 0], -1.0, rstd[:, c % 2, :],
                                               ALU.mult, ALU.mult).then_inc(ln_scale, 1)

            def mask_of(t, u, g):
                if g == 0:
                    dve.wait_ge(adj_loaded[u % 4], (t // 4 + 1) * 16 if is_static(t) else (t - u % 4) * 4 + 16)
                wait(dve, inc_ready, (t - 2) * GROUPS + g + 1)
                nc.vector.tensor_scalar(mask[:, u % 2, g * GW:(g + 1) * GW], adj_t[:, u % 4, g * GW:(g + 1) * GW],
                                        0.0, None, ALU.is_gt).then_inc(mask_ready, 1)

            def head_scale(t, u):
                b = u % 2
                dve.wait_ge(count_ready, (t + 1) * GROUPS)
                nc.vector.tensor_reduce(cnt[:, b:b + 1], cnt4[:, b, :], AX_X, ALU.add).then_inc(cnt_ready, 1)

            def head_scale2(t, u):
                b = u % 2
                dve.wait_ge(root_ready, t + 1)
                nc.vector.tensor_scalar(rclip[:, b:b + 1], root[:, b:b + 1], HEAD_EPS, None, ALU.max).then_inc(rclip_ready, 1)
                dve.wait_ge(rclip_ready, t + 1)
                nc.vector.reciprocal(rinv[:, b:b + 1], rclip[:, b:b + 1]).then_inc(rinv_ready, 1)

            def incidence(t, u, g):
                if g == 0:
                    dve.wait_ge(rinv_ready, t + 1)
                a = adj_t[:, u % 4, g * GW:(g + 1) * GW]
                nc.vector.scalar_tensor_tensor(a, mask[:, u % 2, g * GW:(g + 1) * GW], rinv[:, u % 2:u % 2 + 1], a,
                                               ALU.mult, ALU.add, accum_out=deg4[:, u % 2, g:g + 1]).then_inc(inc_ready, 1)

            def degree(t, u):
                b = u % 2
                dve.wait_ge(inc_ready, (t + 1) * GROUPS)
                nc.vector.tensor_reduce(deg[:, b:b + 1], deg4[:, b, :], AX_X, ALU.add).then_inc(deg_ready, 1)
                dve.wait_ge(deg_ready, t + 1)
                nc.vector.reciprocal(rdeg[:, b:b + 1], deg[:, b:b + 1]).then_inc(rdeg_ready, 1)

            def split_lo(t, u, g):
                dve.wait_ge(hi_ready, t * GROUPS + g + 1)
                nc.vector.tensor_tensor(inc_lo[:, g % 2, :], tr_ps[:, g % 2, :], inc_hi[:, g % 2, :].bitcast(F32),
                                        ALU.subtract).then_inc(lo_ready, 1)

            def residual(t, u):
                b = u % 2
                dve.wait_ge(part_x_ready, t + 1)
                if not is_static(t) or t >= 2:
                    wait(dve, x2_stored[b], (t - b) * 8)
                nc.vector.scalar_tensor_tensor(x2[:, b, :], acc_ps[:, b, 0:D], rdeg[:, b:b + 1], part[:, b, :],
                                               ALU.mult, ALU.add).then_inc(x2_ready, 1)
                dve.wait_ge(x2_ready, t + 1)
                nc.vector.bn_stats(st_b[:], x2[:, b, :]).then_inc(x2_stats, 1)

            def moments(t):
                nc.vector.bn_aggr(mom_b[:], st_b[:]).then_inc(x2_moments, 1)

            def norm_scale(t):
                dve.wait_ge(sd_ready, t + 1)
                nc.vector.tensor_scalar(sd_s[:], sd_b[:], 1.0 / X_SCALE, None, ALU.mult).then_inc(rstd_ready, 1)
                dve.wait_ge(rstd_ready, 2 * t + 1)
                nc.vector.reciprocal(rstd_b[:], sd_s[:]).then_inc(rstd_ready, 1)
                dve.wait_ge(rstd_ready, 2 * t + 2)
                nc.vector.scalar_tensor_tensor(nmr_b[:], mom_b[:, 0:1], -1.0, rstd_b[:], ALU.mult, ALU.mult
                                               ).then_inc(nmr_ready, 1)

            def weight_scale(e, which):
                n = e * 2 + which
                dve.wait_ge(w_rooted, n + 1)
                nc.vector.tensor_scalar(w_norm[:, which, bass.ds(e, 1)], w_root[:], TINY, None, ALU.max).then_inc(w_norm_ready, 1)
                nc.vector.tensor_scalar(w_cut[:], w_root[:], TINY, 1.0 / W_TOP, ALU.max, ALU.mult).then_inc(w_cut_ready, 1)
                dve.wait_ge(w_cut_ready, n + 1)
                nc.vector.reciprocal(w_scale[:], w_cut[:]).then_inc(w_scale_ready, 1)

            def router(t):
                dve.wait_ge(logits_psum, t + 1)
                if is_static(t) and t == 0:
                    dve.wait_ge(consts_loaded, 32)
                lt = logits[:, bass.ds(t, 1), :].rearrange("p o e -> p (o e)")
                nc.vector.scalar_tensor_tensor(lt, lg_ps[:, 0:E], 1.0 / X_SCALE, rb[:], ALU.mult, ALU.add
                                               ).then_inc(logits_ready, 1)

            for g in range(GROUPS):
                mask_of(0, 0, g)
            head_scale(0, 0)
            for g in range(GROUPS):
                mask_of(1, 1, g)
            head_scale2(0, 0)
            for g in range(2):
                incidence(0, 0, g)

            def step(t, u, i):
                behind = lambda k: not is_static(t) or t >= k
                ahead = lambda k: not is_static(t) or t + k < NT
                for g in range(GROUPS):
                    split_lo(t, u, g)
                    if g <= 1:
                        incidence(t, u, g + 2)
                    if g == 0 and behind(3):
                        router(t - 3)
                    if g == 1 and behind(1):
                        residual(t - 1, u - 1)
                    if g == 2 and behind(1):
                        dve.wait_ge(x2_stats, t)
                    if g == 3 and ahead(1):
                        incidence(t + 1, u + 1, 1)
                    if ahead(2):
                        mask_of(t + 2, u + 2, g)
                    if g == 1 and ahead(1):
                        head_scale(t + 1, u + 1)
                    if g == 2:
                        degree(t, u)
                    if g == 2 and ahead(1):
                        head_scale2(t + 1, u + 1)
                        incidence(t + 1, u + 1, 0)
                    if g == 0 and u == 2:
                        weight_scale(i, 0)
                    if g == 0 and u == 0 and (not is_static(i) or i >= 1):
                        weight_scale(i - 1, 1)
                    if g == 2 and behind(1):
                        moments(t - 1)
                    if g == 3 and behind(1):
                        norm_scale(t - 1)

            tiles_looped(dve, step, 1, 1)
            weight_scale(E - 1, 1)
            residual(NT - 1, 3)
            dve.wait_ge(x2_stats, NT)
            moments(NT - 1)
            norm_scale(NT - 1)
            for t in range(NT - 3, NT):
                router(t)
            dve_routing(dve)
            dve_experts(dve)

        @block.tensor
        def _(pe):
            pe.wait_ge(ident_set, 2)

            def transposes(t, u, g):
                wait(pe, inc_ready, t * GROUPS + g + 1)
                wait(pe, lo_ready, t * GROUPS + g - 1)
                for j in range(GJ):
                    m = nc.tensor.transpose(tr_ps[:, g % 2, j * P:(j + 1) * P],
                                            adj_t[:, u % 4, (g * GJ + j) * P:(g * GJ + j + 1) * P], ident[:])
                m.then_inc(transposed, 1)

            def products(t, u, g):
                wait(pe, lo_ready, t * GROUPS + g + 1)
                if is_static(t) and t == 0:
                    pe.wait_ge(cur_ready, (g + 1) * GJ // XCH)
                if g == 0:
                    wait(pe, x2_ready, t - 1)
                acc = acc_ps[:, u % 2, :]
                for j in range(GJ):
                    jc = g * GJ + j

                    def with_hi():
                        return nc.tensor.matmul(acc, inc_hi[:, g % 2, j * P:(j + 1) * P],
                                                cur[:, jc, :, :].rearrange("p h d -> p (h d)"),
                                                start=(jc == 0), stop=(jc == JC - 1))

                    def with_lo():
                        return nc.tensor.matmul(acc[:, 0:D], inc_lo[:, g % 2, j * P:(j + 1) * P], cur[:, jc, 0, :],
                                                start=False, stop=False)

                    if jc == 0:
                        with_hi()
                        m = with_lo()
                    else:
                        with_lo()
                        m = with_hi()
                m.then_inc(multiplied, 1)

            def epilogue_transpose(t, u):
                pe.wait_ge(xn_ready, t + 1)
                wait(pe, xnT_ready, t)
                for c in range(DC):
                    m = nc.tensor.transpose(ep_ps[:, c * P:(c + 1) * P], xn[:, u % 2, c * P:(c + 1) * P], ident[:])
                m.then_inc(xnT_psum, 1)

            def epilogue_logits(t, u):
                pe.wait_ge(xnT_ready, t + 1)
                if is_static(t) and t == 0:
                    pe.wait_ge(consts_loaded, 32)
                wait(pe, logits_ready, t)
                for c in range(DC):
                    m = nc.tensor.matmul(lg_ps[:, 0:E], xnT[:, c, :], rw[:, c, :], start=(c == 0), stop=(c == DC - 1))
                m.then_inc(logits_psum, 1)

            transposes(0, 0, 0)

            def step(t, u, i):
                for g in range(GROUPS):
                    if g + 1 < GROUPS:
                        transposes(t, u, g + 1)
                    elif not is_static(t) or t + 1 < NT:
                        transposes(t + 1, u + 1, 0)
                    if g == 1 and (not is_static(t) or t >= 2):
                        epilogue_transpose(t - 2, u - 2)
                    if g == 3 and (not is_static(t) or t >= 2):
                        epilogue_logits(t - 2, u - 2)
                    products(t, u, g)

            tiles_looped(pe, step, 1, 1)
            for t in (NT - 2, NT - 1):
                epilogue_transpose(t, t % 4)
                epilogue_logits(t, t % 4)
            pe_routing(pe)
            pe_experts(pe)


_INS = ["x", "adj", "L0_ffn_router_w", "L0_ffn_router_b", "L0_ffn_w1", "L0_ffn_b1", "L0_ffn_w2", "L0_ffn_b2"]


def kernel(**inputs):
    import numpy as _np
    import concourse.bacc as _bacc
    from concourse.bass_utils import run_bass_kernel_spmd as _run

    nc = _bacc.Bacc("TRN2", target_bir_lowering=False, num_devices=1)
    arrays, args = {}, []
    for name in _INS:
        a = _np.ascontiguousarray(inputs[name])
        arrays[f"in_{name}_dram"] = a
        args.append(nc.dram_tensor(f"in_{name}_dram", a.shape, mybir.dt.from_np(a.dtype), kind="ExternalInput").ap())
    n, d = inputs["x"].shape
    args.append(nc.dram_tensor("out_0_dram", (n + PAD_ROWS, d), F32, kind="ExternalOutput").ap())
    gnn_moe_kernel(nc, *args)
    r = _run(nc, [arrays], core_ids=[0])
    return r.results[0]["out_0_dram"][:n]
```

```python
from contextlib import ExitStack

import concourse.bass as bass
from concourse import mybir

ALU = mybir.AluOpType
ACT = mybir.ActivationFunctionType
AX_X = mybir.AxisListType.X
F32 = mybir.dt.float32
F32R = mybir.dt.float32r
F16 = mybir.dt.float16
BF16 = mybir.dt.bfloat16
I32 = mybir.dt.int32
U32 = mybir.dt.uint32
RADD = bass.bass_isa.ReduceOp.add

P = 128
LN_EPS = 1e-5
HEAD_EPS = 1e-12
PAD_ROWS = 2 * P
TINY = 1e-30
W_TOP = 2.0 ** 14
H_TOP = 2.0 ** 15
X_SCALE = 256.0


def is_static(v):
    return isinstance(v, int)


def wait(eng, semaphore, value):
    if is_static(value) and value <= 0:
        return
    eng.wait_ge(semaphore, value)


def gnn_moe_kernel(nc, x, adj, router_w, router_b, w1, b1, w2, b2, out):
    N, D = x.shape
    E, _, F = w1.shape
    DC = D // P
    JC = N // P
    NT = N // P
    RING = 4
    GROUPS = 4
    GJ = JC // GROUPS
    GW = GJ * P
    XCH = 4
    XROW = 2 * D + 2 * E

    ctx = ExitStack()
    with ctx:
        def sb(name, shape, dt, stack=ctx):
            return stack.enter_context(nc.sbuf_tensor(name, shape, dt))

        def ps(name, shape, dt, stack=ctx):
            return stack.enter_context(nc.psum_tensor(name, shape, dt))

        def sem(name):
            return ctx.enter_context(nc.semaphore(name))

        W = F * D // P
        WH = W // 2
        FC = F // P
        TT = 2 * P
        EXPERT_TILES = 2 * N // TT + E - 1
        HALVES = 2 * EXPERT_TILES
        LATE = 3
        FULL_TILES = 2 * N // TT
        EARLY = 4
        SLOTS = 2 * NT
        PADS = N + PAD_ROWS

        w_hl = nc.dram_tensor("split_weights", [E, 2, P, 2, W], F16, kind="Internal").ap()
        xtab = nc.dram_tensor("expert_inputs", [N, XROW // 2], U32, kind="Internal").ap()

        logits = sb("logits", [P, NT, E], F32)
        ident = sb("ident", [P, P], F32)
        ident16 = sb("ident16", [P, P], F16)
        w_norm = sb("w_norm", [P, 2, E], F32)
        b_norm = sb("b_norm", [P, E], F32)
        b1t = sb("b1t", [P, E, FC], F32)
        lanes = sb("lanes", [P, P], F32)
        lanes_b = sb("lanes_b", [P, P], BF16)
        lane_col = sb("lane_col", [P, 1], F32)
        order_e = sb("order_e", [P, E], F32)
        tok_hi = sb("tok_hi", [P, 2 * NT], BF16)
        pad_rows = sb("pad_rows", [P, 2], F32)
        earlier = sb("earlier", [P, P], BF16)
        ones_b = sb("ones_b", [P, P], BF16)
        ones_f = sb("ones_f", [P, P], F32)
        ones_row = sb("ones_row", [P, NT * E], F32)

        x_res = sb("x_res", [P, 2, D], F32)
        part = sb("part", [P, 2, D], F32)
        x2 = sb("x2", [P, 2, D], F32)
        xn = sb("xn", [P, 2, D], F32)
        xnT = sb("xnT", [P, DC, P], F32)
        xhl = sb("xhl", [P, 2, 2, D], F16)
        w_sq = sb("w_sq", [P, 2], F32)
        w_sum = sb("w_sum", [P, 1], F32)
        w_tot = sb("w_tot", [P, 1], F32)
        w_root = sb("w_root", [P, 1], F32)
        w_cut = sb("w_cut", [P, 1], F32)
        w_scale = sb("w_scale", [P, 1], F32)

        st2 = ctx.enter_context(ExitStack())
        cur = sb("cur", [P, JC, 2, D], F32R, st2)
        cur32 = cur[:, :, :, :].bitcast(F32)
        adj_t = sb("adj_tiles", [P, RING, N], F32, st2)
        with ExitStack() as st1:
            cur_f = sb("cur_f", [P, 2, XCH, D], F32, st1)
        w_parts = sb("w_parts", [P, 2, W], F16, st2)
        mask = sb("mask", [P, 2, N], BF16, st2)
        inc_hi = sb("inc_hi", [P, 2, GW], F32R, st2)
        inc_lo = sb("inc_lo", [P, 2, GW], F32R, st2)
        stats = sb("stats", [P, 2, XCH, 6], F32, st2)
        mom = sb("mom", [P, 2, XCH, 2], F32, st2)
        sdev = sb("sdev", [P, 2, XCH], F32, st2)
        rstd = sb("rstd", [P, 2, XCH], F32, st2)
        nmr = sb("nmr", [P, 2, XCH // 2], F32, st2)
        eps_c = sb("eps_c", [P, 1], F32, st2)
        eps_row = sb("eps_row", [P, 1], F32, st2)
        eps_head = sb("eps_head", [P, 1], F32, st2)
        rw = sb("rw", [P, DC, E], F32, st2)
        rb = sb("rb", [P, E], F32, st2)
        b1_rows = sb("b1_rows", [E * FC, P], F32, st2)
        b1_sq = sb("b1_sq", [P, E, FC], F32, st2)
        b1_sum = sb("b1_sum", [P, E], F32, st2)
        cnt4 = sb("cnt4", [P, 2, GROUPS], F32, st2)
        cnt = sb("cnt", [P, 2], F32, st2)
        root = sb("root", [P, 2], F32, st2)
        rinv = sb("rinv", [P, 2], F32, st2)
        deg4 = sb("deg4", [P, 2, GROUPS], F32, st2)
        deg = sb("deg", [P, 2], F32, st2)
        rdeg = sb("rdeg", [P, 2], F32, st2)
        st_b = sb("st_b", [P, 6], F32, st2)
        mom_b = sb("mom_b", [P, 2], F32, st2)
        sd_b = sb("sd_b", [P, 1], F32, st2)
        rstd_b = sb("rstd_b", [P, 1], F32, st2)

        with ExitStack() as st1:
            x_in = sb("x_in", [P, 4, XCH, D], F32, st1)
        w_in = sb("w_in", [P, 2, W], F32, st2)
        w_junk = sb("w_junk", [P, WH], BF16, st2)

        tr_ps = ps("tr_ps", [P, 2, GW], F32, st2)
        acc_ps = ps("acc_ps", [P, 2, 2 * D], F32, st2)
        ep_ps = ps("ep_ps", [P, 512], F32, st2)
        lg_ps = ps("lg_ps", [P, 512], F32, st2)

        x_loaded = [sem(f"x_loaded{c}") for c in range(4)]
        adj_loaded = [sem(f"adj_loaded{a}") for a in range(RING)]
        res_loaded = [sem("res_loaded0"), sem("res_loaded1")]
        consts_loaded = sem("consts_loaded")
        ident_set = sem("ident_set")
        eps_set = sem("eps_set")
        constants_set = sem("constants_set")
        pool_waited = sem("pool_waited")
        ln_moments, ln_sdev, ln_scale, ln_scale_r, ln_chain = (
            sem("ln_moments"), sem("ln_sdev"), sem("ln_scale"), sem("ln_scale_r"), sem("ln_chain"))
        cur_f_ready, cur_f_ready_dve, cur_hi_ready, cur_ready = (
            sem("cur_f_ready"), sem("cur_f_ready_dve"), sem("cur_hi_ready"), sem("cur_ready"))
        mask_ready, count_ready, inc_ready = sem("mask_ready"), sem("count_ready"), sem("inc_ready")
        cnt_ready, root_ready, rinv_ready = sem("cnt_ready"), sem("root_ready"), sem("rinv_ready")
        mask_ready_pool = sem("mask_ready_pool")
        transposed, hi_ready, lo_ready, multiplied = sem("transposed"), sem("hi_ready"), sem("lo_ready"), sem("multiplied")
        deg_ready, rdeg_ready, part_ready, part_x_ready = sem("deg_ready"), sem("rdeg_ready"), sem("part_ready"), sem("part_x_ready")
        x2_ready, x2_stats, x2_moments, sd_ready, rstd_ready = (
            sem("x2_ready"), sem("x2_stats"), sem("x2_moments"), sem("sd_ready"), sem("rstd_ready"))
        xn_ready, xhi_ready, xlo_ready, xnT_psum, xnT_ready = (
            sem("xn_ready"), sem("xhi_ready"), sem("xlo_ready"), sem("xnT_psum"), sem("xnT_ready"))
        logits_psum, logits_ready = sem("logits_psum"), sem("logits_ready")
        x2_stored = [sem("x2_stored0"), sem("x2_stored1")]
        xhl_stored = [sem("xhl_stored0"), sem("xhl_stored1")]

        w_loaded = [sem("w1_loaded"), sem("w2_loaded")]
        w_squared, w_summed, w_total, w_rooted, w_norm_ready, w_cut_ready, w_scale_ready = (
            sem("w_squared"), sem("w_summed"), sem("w_total"), sem("w_rooted"), sem("w_norm_ready"), sem("w_cut_ready"),
            sem("w_scale_ready"))
        w_hi_ready, w_scaled, w_parted, w_stored = sem("w_hi_ready"), sem("w_scaled"), sem("w_parted"), sem("w_stored")
        rows_stored = sem("rows_stored")

        st2.close()
        w_res = sb("w_resident", [P, E, 2, 2, W], F16)
        b2_all = sb("b2_all", [P, E, D], F32)
        bound = sb("bound", [P, E], F32)
        bound_c = sb("bound_c", [P, E], F32)
        h_scale = sb("h_scale", [P, E], F32)
        best = sb("best", [P, 2, NT], F32)
        equal = sb("equal", [P, NT, E], F32)
        ranked = sb("ranked", [P, NT, E], F32)
        first = sb("first", [P, NT], F32)
        rest = sb("rest", [P, NT, E], F32)
        chosen = sb("chosen", [P, 2, NT, E], F32)
        ch = sb("relu_scale", [P, E], F32)
        c2 = sb("out_scale", [P, E], F32)
        b1s = sb("b1_scaled", [P, E, FC], F32)
        gather_idx = sb("gather_idx", [P, EXPERT_TILES, 2], U32)
        scatter_idx = sb("scatter_idx", [P, EXPERT_TILES, 2], U32)
        tile_expert = sb("tile_expert", [P, EXPERT_TILES], I32)
        tiles_used = sb("tiles_used", [P, 1], I32)

        st3 = ctx.enter_context(ExitStack())
        zero_rows = sb("zero_rows", [P, 2, D], F32, st3)
        either = sb("either", [P, E, NT], BF16, st3)
        gap = sb("gap", [P, NT], F32, st3)
        gap_exp = sb("gap_exp", [P, NT], F32, st3)
        gate_den = sb("gate_den", [P, NT], F32, st3)
        gate = sb("gate", [P, 2, NT], F32, st3)
        gated = sb("gated", [P, 2, NT, E], F32, st3)
        comb = sb("comb", [P, NT, E], F32, st3)
        running = sb("running", [P, E, NT], F32, st3)
        before = sb("before", [P, E, NT], F32, st3)
        n_tok = sb("n_tok", [P, E], F32, st3)
        n_pad = sb("n_pad", [P, E], I32, st3)
        n_tiles_i = sb("n_tiles_i", [P, E], I32, st3)
        tile_end = sb("tile_end", [P, E], F32, st3)
        tile_start = sb("tile_start", [P, E], F32, st3)
        offset = sb("offset", [P, E], F32, st3)
        place = sb("place", [P, E, NT], F32, st3)
        place2 = sb("place2", [P, E, NT], F32, st3)
        picked = sb("picked", [P, 2, NT, E], F32, st3)
        slot = sb("slot", [P, 2, NT], F32, st3)
        slot_i = sb("slot_i", [P, SLOTS], I32, st3)
        slot_hi_i = sb("slot_hi_i", [P, SLOTS], I32, st3)
        slot_lo_i = sb("slot_lo_i", [P, SLOTS], I32, st3)
        QS = SLOTS // 4
        lane_hot = sb("lane_hot", [P, 2, QS, P], BF16, st3)
        half_hot = sb("half_hot", [P, 2, QS, HALVES], BF16, st3)
        half_val = sb("half_val", [P, 2, QS, 2, HALVES], BF16, st3)
        ended = sb("ended", [P, EXPERT_TILES, E], F32, st3)
        n_ended = sb("n_ended", [P, EXPERT_TILES], F32, st3)
        rank_ps = ps("rank_ps", [P, 512], F32, st3)
        total_ps = ps("total_ps", [P, 512], F32, st3)
        idx_ps = ps("idx_ps", [P, 512], F32, st3)
        st3.close()

        x_g = sb("x_gathered", [P, 2, 2, XROW // 2], U32)
        g_idx = sb("g_idx", [P, 2, 2], U32)
        s_idx = sb("s_idx", [P, 2, 2], U32)
        x_t = sb("x_t", [P, 2, DC, TT], F16)
        tile_gate = sb("tile_gate", [P, 2, 2], F32)
        h_f = sb("h_f", [P, FC, TT], F32)
        h_hl = sb("h_hl", [P, 2, 2, FC, TT], F16)
        y1 = sb("y1", [P, 2, D], F32)
        y = sb("y", [P, 2, 2, D], F32)
        xt_ps = ps("xt_ps", [P, 2, DC, TT], F16)
        h_ps = ps("h_ps", [P, FC, TT], F32)
        y_ps = ps("y_ps", [P, 2, 2, D], F32)

        b1_loaded, b2_loaded, comb_stored, pads_cleared = sem("b1_loaded"), sem("b2_loaded"), sem("comb_stored"), sem("pads_cleared")
        b1_turned, b1_squared, b1_summed, b1_rooted = sem("b1_turned"), sem("b1_squared"), sem("b1_summed"), sem("b1_rooted")
        zeroed = sem("zeroed")
        route = sem("route")
        scatter_ready, gates_ready, gated_ready, half_hi_ready, hot_used, scaled = (
            sem("scatter_ready"), sem("gates_ready"), sem("gated_ready"), sem("half_hi_ready"), sem("hot_used"), sem("scaled"))
        chosen_ready, ranks_ready, gap_ready, gap_exp_ready, comb_ready = (
            sem("chosen_ready"), sem("ranks_ready"), sem("gap_ready"), sem("gap_exp_ready"), sem("comb_ready"))
        hot_ready, half_ready, half_lo_ready, idx_summed, routed = (
            sem("hot_ready"), sem("half_ready"), sem("half_lo_ready"), sem("idx_summed"), sem("routed"))
        w_arrived = [sem("w_arrived0"), sem("w_arrived1")]
        w_resident = sem("w_resident_experts")
        idx_copied = sem("idx_copied")
        gathered = [sem("gathered0"), sem("gathered1")]
        x_turned, x_t_ready, gate_copied = sem("x_turned"), sem("x_t_ready"), sem("gate_copied")
        product1, relu_ready, h_hi_ready, h_lo_ready = sem("product1"), sem("relu_ready"), sem("h_hi_ready"), sem("h_lo_ready")
        product2, y1_ready, y_ready = sem("product2"), sem("y1_ready"), sem("y_ready")
        s_idx_copied, scattered = sem("s_idx_copied"), sem("scattered")

        def spread(ap, shape):
            return ap.broadcast_to(shape)

        def experts_looped(eng, step):
            always = lambda s: ExitStack()
            for s in range(3):
                step(s, s % 2, always)
            with eng.Fori(0, (FULL_TILES - 4) // 2) as i:
                step(i * 2 + 3, 1, always)
                step(i * 2 + 4, 0, always)
            used = eng.value_load(tiles_used[0:1, 0:1], min_val=FULL_TILES, max_val=EXPERT_TILES)
            asked = lambda s: eng.If(used > s) if s >= FULL_TILES else ExitStack()
            for s in range(FULL_TILES - 1, EXPERT_TILES):
                step(s, s % 2, asked)
            return asked

        def resident_weights(sp):
            def load(e):
                sp.dma_start(w_res[:, e, :, :, :].rearrange("p m h w -> p m (h w)"), w_hl[e].rearrange("m p h w -> p m (h w)")
                             ).then_inc(w_arrived[e % 2], 16)

            def arrived(e):
                sp.wait_ge(w_arrived[e % 2], 16 * (e // 2 + 1))
                sp.sem_inc(w_resident, 1)

            sp.wait_ge(multiplied, GROUPS * NT)
            sp.wait_ge(w_stored, 16 * 2 * (E - 2))
            for e in range(EARLY):
                load(e)
                if e >= 1:
                    arrived(e - 1)
                if e == 1:
                    sp.wait_ge(zeroed, 1)
                    sp.dma_start(out[N:PADS, :].rearrange("(h p) d -> p h d", p=P), zero_rows[:]).then_inc(pads_cleared, 16)
                    sp.wait_ge(w_parted, 4 * E)
                    sp.dma_start(w_hl[E - 1, 1].rearrange("p h w -> p (h w)"), w_parts[:].rearrange("p h w -> p (h w)")
                                 ).then_inc(w_stored, 16)
                    sp.wait_ge(comb_ready, 1)
                    sp.dma_start(xtab[:, D:D + E].rearrange("(t p) e -> p t e", p=P), comb[:].bitcast(U32)
                                 ).then_inc(comb_stored, 16)
            arrived(EARLY - 1)
            sp.wait_ge(w_stored, 16 * 2 * E)
            sp.dma_start(b2_all[:].rearrange("p e d -> p (e d)"),
                         b2.rearrange("(o e) d -> o (e d)", o=1).broadcast_to([P, E * D])).then_inc(b2_loaded, 16)
            sp.wait_ge(gathered[1], 32)
            for e in range(EARLY, E):
                load(e)
                arrived(e)
            sp.wait_ge(comb_stored, 16)
            sp.wait_ge(pads_cleared, 16)

        steps = [0]

        def put(ins):
            steps[0] += 1
            ins.then_inc(route, 1)

        def settle():
            nc.vector.wait_ge(route, steps[0])

        def link(ins):
            put(ins)
            settle()

        def top_two(dve, t0, t1):
            V = nc.vector
            shape = [P, t1 - t0, E]
            ts = slice(t0, t1)
            dve.wait_ge(logits_ready, t1)
            for k in range(2):
                src = logits if k == 0 else rest
                link(V.tensor_reduce(best[:, k, ts], src[:, ts, :], AX_X, ALU.max))
                link(V.tensor_tensor(equal[:, ts, :], src[:, ts, :], spread(best[:, k, ts].rearrange("p (t o) -> p t o", o=1), shape),
                                     ALU.is_equal))
                link(V.tensor_tensor(ranked[:, ts, :], equal[:, ts, :], spread(order_e[:].rearrange("p (o e) -> p o e", o=1), shape),
                                     ALU.mult))
                link(V.tensor_reduce(first[:, ts], ranked[:, ts, :], AX_X, ALU.max))
                link(V.tensor_tensor(chosen[:, k, ts, :], ranked[:, ts, :], spread(first[:, ts].rearrange("p (t o) -> p t o", o=1), shape),
                                     ALU.is_equal))
                if k == 0:
                    link(V.scalar_tensor_tensor(rest[:, ts, :], chosen[:, 0, ts, :], -3.0e38, logits[:, ts, :], ALU.mult, ALU.add))

        def dve_routing(dve):
            V = nc.vector
            top_two(dve, NT - LATE, NT)
            dve.wait_ge(multiplied, GROUPS * NT)
            V.tensor_tensor(either[:].rearrange("p e t -> p t e"), chosen[:, 0, :, :], chosen[:, 1, :, :], ALU.add).then_inc(chosen_ready, 1)
            V.tensor_tensor(gap[:], best[:, 1, :], best[:, 0, :], ALU.subtract).then_inc(gap_ready, 1)
            dve.wait_ge(ranks_ready, 1)
            totals = total_ps[:, 0:NT * E].rearrange("p (e t) -> p e t", e=E)
            flat = lambda a: a[:].rearrange("p e t -> p (e t)")
            link(V.tensor_tensor_scan(flat(running), ones_row[:, 0:NT * E], total_ps[:, 0:NT * E], 0.0, ALU.mult, ALU.add))
            dve.wait_ge(gap_exp_ready, 1)
            put(V.tensor_scalar(gate_den[:], gap_exp[:], 1.0, None, ALU.add))
            link(V.tensor_tensor(before[:], running[:], totals, ALU.subtract))
            put(V.reciprocal(gate[:, 0, :], gate_den[:]))
            link(V.tensor_tensor(n_tok[:], running[:, :, NT - 1], before[:, :, 0], ALU.subtract))
            V.tensor_tensor(gate[:, 1, :], gate[:, 0, :], gap_exp[:], ALU.mult).then_inc(gates_ready, 1)
            link(V.tensor_scalar(n_pad[:], n_tok[:], float(TT - 1), None, ALU.add))
            put(V.tensor_scalar(n_tiles_i[:], n_pad[:], 8, None, ALU.arith_shift_right))
            link(V.tensor_tensor(place[:], rank_ps[:, 0:NT * E].rearrange("p (e t) -> p e t", e=E), before[:], ALU.add))
            link(V.tensor_tensor_scan(tile_end[:], ones_row[:, 0:E], n_tiles_i[:], 0.0, ALU.mult, ALU.add))
            link(V.tensor_tensor(tile_start[:], tile_end[:], n_tiles_i[:], ALU.subtract))
            link(V.scalar_tensor_tensor(offset[:], tile_start[:], float(TT), before[:, :, 0], ALU.mult, ALU.subtract))
            link(V.tensor_tensor(place2[:], place[:], spread(offset[:].rearrange("p (e o) -> p e o", o=1), [P, E, NT]), ALU.add))
            for k in range(2):
                put(V.tensor_tensor(picked[:, k, :, :], place2[:].rearrange("p e t -> p t e"), chosen[:, k, :, :], ALU.mult))
            settle()
            link(V.tensor_reduce(slot[:], picked[:], AX_X, ALU.add))
            link(V.tensor_copy(slot_i[:], slot[:].rearrange("p k t -> p (k t)")))
            put(V.tensor_scalar(slot_lo_i[:], slot_i[:], P - 1, None, ALU.bitwise_and))
            link(V.tensor_scalar(slot_hi_i[:], slot_i[:], 7, None, ALU.arith_shift_right))
            dve.wait_ge(w_parted, 4 * E)
            for q in range(4):
                if q >= 2:
                    dve.wait_ge(hot_used, q - 1)
                js = slice(q * QS, (q + 1) * QS)
                V.tensor_tensor(half_hot[:, q % 2, :, :], spread(lanes_b[:, 0:HALVES].rearrange("p (o h) -> p o h", o=1), [P, QS, HALVES]),
                                spread(slot_hi_i[:, js].rearrange("p (j o) -> p j o", o=1), [P, QS, HALVES]), ALU.is_equal
                                ).then_inc(half_ready, 1)
                V.tensor_tensor(lane_hot[:, q % 2, :, :], spread(lanes_b[:].rearrange("p (o h) -> p o h", o=1), [P, QS, P]),
                                spread(slot_lo_i[:, js].rearrange("p (j o) -> p j o", o=1), [P, QS, P]), ALU.is_equal
                                ).then_inc(hot_ready, 1)
            link(V.tensor_tensor(ended[:], spread(tile_end[:].rearrange("p (o e) -> p o e", o=1), [P, EXPERT_TILES, E]),
                                 spread(lanes[:, 0:EXPERT_TILES].rearrange("p (j o) -> p j o", o=1), [P, EXPERT_TILES, E]), ALU.is_le))
            link(V.tensor_reduce(n_ended[:], ended[:], AX_X, ALU.add))
            put(V.tensor_scalar(tile_expert[:], n_ended[:], float(E - 1), None, ALU.min))
            link(V.tensor_copy(tiles_used[:], tile_end[:, E - 1:E]))
            dve.wait_ge(idx_summed, 1)
            token = idx_ps[:, 0:HALVES].rearrange("p (j h) -> p j h", h=2)
            link(V.tensor_scalar(gather_idx[:], token, 2.0 * N, float(N - 1), ALU.add, ALU.min))
            dve.sem_inc(routed, 1)
            link(V.scalar_tensor_tensor(scatter_idx[:], token, 2.0 * N, spread(pad_rows[:].rearrange("p (o h) -> p o h", o=1),
                                                                                  [P, EXPERT_TILES, 2]), ALU.add, ALU.min))
            dve.sem_inc(scatter_ready, 1)
            dve.wait_ge(b1_rooted, 1)
            link(V.scalar_tensor_tensor(bound[:], w_norm[:, 0, :], float(D) ** 0.5, b_norm[:], ALU.mult, ALU.add))
            link(V.tensor_scalar(bound_c[:], bound[:], TINY, 1.0 / H_TOP, ALU.max, ALU.mult))
            link(V.reciprocal(h_scale[:], bound_c[:]))
            put(V.scalar_tensor_tensor(ch[:], h_scale[:], 1.0 / (X_SCALE * W_TOP), w_norm[:, 0, :], ALU.mult, ALU.mult))
            put(V.tensor_tensor(b1s[:], b1t[:], spread(h_scale[:].rearrange("p (e o) -> p e o", o=1), [P, E, FC]), ALU.mult))
            link(V.scalar_tensor_tensor(c2[:], bound_c[:], 1.0 / W_TOP, w_norm[:, 1, :], ALU.mult, ALU.mult))
            dve.sem_inc(scaled, 1)

        def pe_routing(pe):
            pe.wait_ge(chosen_ready, 1)
            sel = either[:].rearrange("p e t -> p (e t)")
            nc.tensor.matmul(rank_ps[:, 0:NT * E], earlier[:], sel, start=True, stop=True)
            nc.tensor.matmul(total_ps[:, 0:NT * E], ones_b[:], sel, start=True, stop=True).then_inc(ranks_ready, 1)
            for q in range(4):
                pe.wait_ge(hot_ready, q + 1)
                pe.wait_ge(half_lo_ready, q + 1)
                pe.wait_ge(half_hi_ready, q + 1)
                for j in range(QS):
                    for v in range(2):
                        m = nc.tensor.matmul(idx_ps[:, 0:HALVES], lane_hot[:, q % 2, j, :], half_val[:, q % 2, j, v, :],
                                             start=(q == 0 and j == 0 and v == 0), stop=(q == 3 and j == QS - 1 and v == 1))
                m.then_inc(hot_used if q < 3 else idx_summed, 1)

        def act_routing(act):
            act.wait_ge(gap_ready, 1)
            nc.scalar.activation(gap_exp[:], gap[:], ACT.Exp).then_inc(gap_exp_ready, 1)
            for q in range(4):
                act.wait_ge(half_ready, q + 1)
                if q >= 2:
                    act.wait_ge(hot_used, q - 1)
                nc.scalar.activation(half_val[:, q % 2, :, 1, :], half_hot[:, q % 2, :, :], ACT.Copy, scale=lane_col[:, 0:1]
                                     ).then_inc(half_lo_ready, 1)

        def pool_routing(pool):
            pool.wait_ge(gates_ready, 1)
            for k in range(2):
                nc.gpsimd.tensor_tensor(gated[:, k, :, :], chosen[:, k, :, :],
                                        spread(gate[:, k, :].rearrange("p (t o) -> p t o", o=1), [P, NT, E]), ALU.mult
                                        ).then_inc(gated_ready, 1)
            pool.wait_ge(gated_ready, 2)
            nc.gpsimd.tensor_tensor(comb[:], gated[:, 0, :, :], gated[:, 1, :, :], ALU.add).then_inc(comb_ready, 1)
            for q in range(4):
                pool.wait_ge(half_ready, q + 1)
                if q >= 2:
                    pool.wait_ge(hot_used, q - 1)
                nc.gpsimd.tensor_tensor(half_val[:, q % 2, :, 0, :], half_hot[:, q % 2, :, :],
                                        spread(tok_hi[:, q * QS:(q + 1) * QS].rearrange("p (j o) -> p j o", o=1), [P, QS, HALVES]),
                                        ALU.mult).then_inc(half_hi_ready, 1)

        def tile_e(eng, s):
            return eng.value_load(tile_expert[0:1, bass.ds(s, 1)], min_val=0, max_val=E - 1)

        def pe_experts(pe):
            pe.wait_ge(routed, 1)

            def turn(s, u):
                wait(pe, gathered[u], (s // 2 + 1) * 32 if is_static(s) else (s - u) * 16 + 32)
                wait(pe, x_t_ready, s)
                for hl in range(2):
                    for c in range(DC):
                        for half in range(2):
                            m = nc.tensor.transpose(xt_ps[:, hl, c, half * P:(half + 1) * P],
                                                    x_g[:, u, half, :].bitcast(F16)[:, hl * D + c * P:hl * D + (c + 1) * P], ident16[:])
                m.then_inc(x_turned, 1)

            def first_product(s, u):
                e = tile_e(pe, s)
                pe.wait_ge(w_resident, e + 1)
                pe.wait_ge(x_t_ready, s + 1)
                for f in range(FC):
                    if f % 2 == 0:
                        wait(pe, relu_ready, (s - 1) * FC + f + 2)
                    o = h_ps[:, f, :]
                    n = 0
                    for wh, xh in ((0, 0), (0, 1), (1, 0)):
                        for c in range(DC):
                            m = nc.tensor.matmul(o, w_res[:, bass.ds(e, 1), 0, wh, c * F + f * P:c * F + (f + 1) * P
                                                          ].rearrange("p o f -> p (o f)"),
                                                 x_t[:, xh, c, :], start=(n == 0), stop=(n == 3 * DC - 1))
                            n += 1
                    if f % 2 == 1:
                        m.then_inc(product1, 1)

            def second_product(s, u):
                e = tile_e(pe, s)
                pe.wait_ge(h_lo_ready, s * 2 + 2)
                wait(pe, y1_ready, s - 1)
                for half in range(2):
                    n = 0
                    for f in range(FC):
                        for hh, wh in ((0, 0), (1, 0), (0, 1)):
                            m = nc.tensor.matmul(y_ps[:, u, half, :], h_hl[:, u, hh, f, half * P:(half + 1) * P],
                                                 w_res[:, bass.ds(e, 1), 1, wh, f * D:(f + 1) * D].rearrange("p o d -> p (o d)"),
                                                 start=(n == 0), stop=(n == 3 * FC - 1))
                            n += 1
                m.then_inc(product2, 1)

            def step(s, u, has):
                with has(s):
                    turn(s, u)
                if not is_static(s) or s >= 2:
                    with has(s - 2):
                        second_product(s - 2, u)
                with has(s):
                    first_product(s, u)

            has = experts_looped(pe, step)
            for s in (EXPERT_TILES - 2, EXPERT_TILES - 1):
                with has(s):
                    second_product(s, s % 2)

        def act_experts(act):
            act.wait_ge(routed, 1)
            act.wait_ge(scaled, 1)

            def hidden(s, u):
                e = tile_e(act, s)
                for f in range(FC):
                    if f % 2 == 0:
                        act.wait_ge(product1, s * (FC // 2) + f // 2 + 1)
                    if f % (FC // 2) == 0:
                        wait(act, h_lo_ready, (s - 1) * 2 + f // (FC // 2) + 1)
                    nc.scalar.activation(h_f[:, f, :], h_ps[:, f, :], ACT.Relu, bias=b1s[:, bass.ds(e, 1), f],
                                         scale=ch[:, bass.ds(e, 1)]).then_inc(relu_ready, 1)
                    if f % (FC // 2) == FC // 2 - 1:
                        act.wait_ge(relu_ready, s * FC + f + 1)
                        if f < FC // 2:
                            wait(act, product2, s - 1)
                        fs = slice(f + 1 - FC // 2, f + 1)
                        nc.scalar.activation(h_hl[:, u, 0, fs, :], h_f[:, fs, :], ACT.Copy).then_inc(h_hi_ready, 1)

            def step(s, u, has):
                with has(s):
                    hidden(s, u)

            experts_looped(act, step)

        def dve_experts(dve):

            def combine(s, u):
                e = tile_e(dve, s)
                dve.wait_ge(product2, s + 1)
                if is_static(s) and s == 0:
                    dve.wait_ge(b2_loaded, 16)
                wait(dve, y_ready, s)
                nc.vector.scalar_tensor_tensor(y1[:], y_ps[:, u, :, :], c2[:, bass.ds(e, 1)],
                                               spread(b2_all[:, bass.ds(e, 1), :], [P, 2, D]), ALU.mult, ALU.add
                                               ).then_inc(y1_ready, 1)
                dve.wait_ge(y1_ready, s + 1)
                wait(dve, scattered, (s - 1) * 32)
                for half in range(2):
                    m = nc.vector.tensor_scalar(y[:, u, half, :], y1[:, half, :], tile_gate[:, u, half:half + 1], None, ALU.mult)
                m.then_inc(y_ready, 1)

            def take_rows(s, u, has):
                with has(s):
                    dve.wait_ge(x_turned, s + 1)
                    flat4 = lambda a: a.rearrange("p h c t -> p (h c t)")
                    nc.vector.tensor_copy(flat4(x_t[:]), flat4(xt_ps[:])).then_inc(x_t_ready, 1)
                if not is_static(s) or s >= 2:
                    with has(s - 2):
                        combine(s - 2, u)
                with has(s):
                    e = tile_e(dve, s)
                    wait(dve, y_ready, s - 1)
                    nc.vector.tensor_copy(tile_gate[:, u, :].rearrange("p (h o) -> p h o", o=1),
                                          x_g[:, u, :, :].bitcast(F32)[:, :, bass.ds(e + D, 1)]).then_inc(gate_copied, 1)

            def split_hidden(s, u):
                for h in range(2):
                    dve.wait_ge(h_hi_ready, s * 2 + h + 1)
                    fs = slice(h * FC // 2, (h + 1) * FC // 2)
                    nc.vector.tensor_tensor(h_hl[:, u, 1, fs, :], h_f[:, fs, :], h_hl[:, u, 0, fs, :], ALU.subtract
                                            ).then_inc(h_lo_ready, 1)

            def step(s, u, has):
                if is_static(s) and s == 0:
                    take_rows(0, 0, has)
                    take_rows(1, 1, has)
                elif not is_static(s) or s >= 2:
                    take_rows(s, u, has)
                with has(s):
                    split_hidden(s, u)

            has = experts_looped(dve, step)
            for s in (EXPERT_TILES - 2, EXPERT_TILES - 1):
                with has(s):
                    combine(s, s % 2)

        def pool_experts(pool):
            pool_routing(pool)
            pool.wait_ge(routed, 1)
            pool.wait_ge(rows_stored, 1)
            pool.wait_ge(comb_stored, 16)
            pool.wait_ge(pads_cleared, 16)

            def gather(s, u):
                wait_apart(pool, gate_copied, s - 1)
                wait_apart(pool, x_turned, s - 1)
                nc.gpsimd.tensor_copy(g_idx[:, u, :], gather_idx[:, bass.ds(s, 1), :].rearrange("p o h -> p (o h)")
                                      ).then_inc(idx_copied, 1)
                wait_apart(pool, idx_copied, s + 1)
                for half in range(2):
                    nc.gpsimd.indirect_dma_start(x_g[:, u, half, :], None, xtab[:, :],
                                                 bass.IndirectOffsetOnAxis(ap=g_idx[:, u, half:half + 1], axis=0)
                                                 ).then_inc(gathered[u], 16)

            def scatter(s, u):
                wait_apart(pool, scattered, s * 32)
                nc.gpsimd.tensor_copy(s_idx[:, u, :], scatter_idx[:, bass.ds(s, 1), :].rearrange("p o h -> p (o h)")
                                      ).then_inc(s_idx_copied, 1)
                wait_apart(pool, s_idx_copied, s + 1)
                wait_apart(pool, y_ready, s + 1)
                for half in range(2):
                    nc.gpsimd.indirect_dma_start(out[:, :], bass.IndirectOffsetOnAxis(ap=s_idx[:, u, half:half + 1], axis=0),
                                                 y[:, u, half, :], None, compute_op=ALU.add).then_inc(scattered, 16)

            def step(s, u, has):
                with has(s):
                    gather(s, u)
                if not is_static(s) or s >= 3:
                    with has(s - 3):
                        scatter(s - 3, (u + 1) % 2)

            pool.wait_ge(scatter_ready, 1)
            has = experts_looped(pool, step)
            for s in range(EXPERT_TILES - 3, EXPERT_TILES):
                with has(s):
                    scatter(s, s % 2)
            pool.wait_ge(scattered, FULL_TILES * 32)
            for s in range(FULL_TILES, EXPERT_TILES):
                with has(s):
                    pool.wait_ge(scattered, (s + 1) * 32)
                    pool.sem_inc(pool_waited, 1)

        block = ctx.enter_context(nc.Block())

        def masks_dve(t, g):
            return 4 * t + g + 1 if is_static(t) and t < 2 else t * 2 + (g + 5)

        def wait_mask(eng, t, g):
            if g < 2 or (is_static(t) and t < 2):
                eng.wait_ge(mask_ready, masks_dve(t, g))
            else:
                eng.wait_ge(mask_ready_pool, t * 2 + (g - 5))

        def tiles_looped(eng, step, first, last):
            for i in range(first):
                for u in range(4):
                    step(4 * i + u, u, i)
            with eng.Fori(first, NT // 4 - last) as i:
                for u in range(4):
                    step(i * 4 + u, u, i)
            for i in range(NT // 4 - last, NT // 4):
                for u in range(4):
                    step(4 * i + u, u, i)

        @block.sync
        def _(sp):
            def load_x(c):
                if c >= 4:
                    sp.wait_ge(cur_hi_ready, c - 3)
                sp.dma_start(x_in[:, c % 4, :, :], x[c * XCH * P:(c + 1) * XCH * P, :].rearrange("(t p) d -> p t d", p=P)
                             ).then_inc(x_loaded[c % 4], 16)

            def load_adj(t, u):
                wait(sp, transposed, GROUPS * (t - RING) + GROUPS)
                sp.dma_start(adj_t[:, u, :], adj[bass.ds(t * P, P), :]).then_inc(adj_loaded[u], 16)

            def load_res(t, u):
                wait(sp, part_x_ready, t - 1)
                sp.dma_start(x_res[:, u % 2, :], x[bass.ds(t * P, P), :]).then_inc(res_loaded[u % 2], 16)

            def load_weights(e, which):
                n = e * 2 + which
                if is_static(n) and n == 0:
                    sp.wait_ge(cur_ready, NT // XCH)
                wait(sp, w_parted, (n - 2) * 2 + 2)
                src = (w1[bass.ds(e, 1), :, :].rearrange("o (c p) f -> p (o c) f", p=P) if which == 0 else
                       w2[bass.ds(e, 1), :, :].rearrange("o (c p) d -> p (o c) d", p=P))
                sp.dma_start(w_in[:, which, :].rearrange("p (c f) -> p c f", c=DC if which == 0 else FC), src
                             ).then_inc(w_loaded[which], 16)

            def store_weights(e, which):
                sp.wait_ge(w_parted, (e * 2 + which) * 2 + 2)
                sp.dma_start(w_hl[bass.ds(e, 1), which, :, :, :].rearrange("o p h w -> p (o h) w"), w_parts[:]
                             ).then_inc(w_stored, 16)

            def step(t, u, i):
                if not is_static(t) or t + 3 < NT:
                    load_adj(t + 3, (u + 3) % 4)
                load_res(t, u)
                if u % 2 == 0:
                    if not is_static(i) or i >= 1:
                        store_weights(i - 1, u // 2)
                    load_weights(i, u // 2)

            for c in range(2):
                load_x(c)
            load_adj(0, 0)
            for c in range(2, NT // XCH):
                load_x(c)
            load_adj(1, 1)
            load_adj(2, 2)
            tiles_looped(sp, step, 1, 1)
            store_weights(E - 1, 0)
            resident_weights(sp)

        def wait_apart(pool, semaphore, value):
            if is_static(value) and value <= 0:
                return
            pool.wait_ge(semaphore, value)
            pool.sem_inc(pool_waited, 1)

        @block.gpsimd
        def _(pool):
            nc.gpsimd.memset(ident[:], 0.0).then_inc(ident_set, 1)
            pool.wait_ge(ident_set, 1)
            nc.gpsimd.affine_select(out=ident[:], in_=ident[:], compare_op=ALU.not_equal, fill=1.0, base=0,
                                    pattern=[[-1, P]], channel_multiplier=1).then_inc(ident_set, 1)

            def numbers(a, pattern, base, across):
                nc.gpsimd.iota(a, pattern, base=base, channel_multiplier=across, allow_small_or_imprecise_dtypes=True
                               ).then_inc(constants_set, 1)

            pool.wait_ge(ident_set, 2)
            nc.gpsimd.tensor_copy(ident16[:], ident[:]).then_inc(constants_set, 1)
            numbers(lanes[:], [[1, P]], 0, 0)
            numbers(lanes_b[:], [[1, P]], 0, 0)
            numbers(lane_col[:], [[0, 1]], 0, 1)
            numbers(order_e[:], [[-1, E]], E, 0)
            numbers(tok_hi[:], [[0, 2], [P, NT]], -2 * N, 0)
            numbers(pad_rows[:], [[P, 2]], N, 1)
            nc.gpsimd.memset(ones_b[:], 1.0).then_inc(constants_set, 1)
            nc.gpsimd.memset(ones_f[:], 1.0).then_inc(constants_set, 1)
            nc.gpsimd.memset(ones_row[:], 1.0).then_inc(constants_set, 1)
            pool.wait_ge(constants_set, 10)
            nc.gpsimd.affine_select(out=earlier[:], in_=ones_b[:], compare_op=ALU.is_gt, fill=0.0, base=0,
                                    pattern=[[1, P]], channel_multiplier=-1).then_inc(constants_set, 1)

            for c in range(NT // XCH):
                pool.wait_ge(cur_hi_ready, c + 1)
                nc.gpsimd.tensor_tensor(cur[:, c * XCH:(c + 1) * XCH, 1, :], cur_f[:, c % 2, :, :],
                                        cur32[:, c * XCH:(c + 1) * XCH, 0, :], ALU.subtract).then_inc(cur_ready, 1)

            def sum_squares(e, which):
                n = e * 2 + which
                pool.wait_ge(w_squared, n * 2 + 2)
                nc.gpsimd.tensor_tensor(w_sum[:], w_sq[:, 0:1], w_sq[:, 1:2], ALU.add).then_inc(w_summed, 1)
                wait_apart(pool, w_summed, n + 1)
                nc.gpsimd.partition_all_reduce(w_tot[:], w_sum[:], P, RADD).then_inc(w_total, 1)

            def split_weights(e, which):
                n = e * 2 + which
                for h in range(2):
                    cols = slice(h * WH, (h + 1) * WH)
                    wait_apart(pool, w_hi_ready, n * 2 + h + 1)
                    nc.gpsimd.tensor_tensor(w_parts[:, 1, cols], w_in[:, which, cols], w_parts[:, 0, cols], ALU.subtract
                                            ).then_inc(w_parted, 1)

            def mask_of(t, u, g):
                wait_apart(pool, inc_ready, (t - 2) * GROUPS + g + 1)
                if g == 2:
                    wait_apart(pool, adj_loaded[u % 4], (t // 4 + 1) * 16 if is_static(t) else (t - u % 4) * 4 + 16)
                nc.gpsimd.tensor_scalar(mask[:, u % 2, g * GW:(g + 1) * GW], adj_t[:, u % 4, g * GW:(g + 1) * GW],
                                        0.0, None, ALU.is_gt).then_inc(mask_ready_pool, 1)

            def epilogue(t, u):
                pool.wait_ge(part_ready, t + 1)
                wait(pool, res_loaded[u % 2], (t // 2 + 1) * 16 if is_static(t) else ((t - u % 2) * 8 + 16))
                nc.gpsimd.tensor_tensor(part[:, u % 2, :], part[:, u % 2, :], x_res[:, u % 2, :], ALU.add
                                        ).then_inc(part_x_ready, 1)

            def low(t, u):
                pool.wait_ge(xhi_ready, t + 1)
                nc.gpsimd.tensor_tensor(xhl[:, u % 2, 1, :], xn[:, u % 2, :], xhl[:, u % 2, 0, :], ALU.subtract
                                        ).then_inc(xlo_ready, 1)

            def step(t, u, i):
                epilogue(t, u)
                if u % 2 == 1:
                    sum_squares(i, u // 2)
                if not is_static(t) or t + 3 < NT:
                    mask_of(t + 3, u + 3, 2)
                if not is_static(t) or t >= 1:
                    low(t - 1, u - 1)
                if not is_static(t) or t + 3 < NT:
                    mask_of(t + 3, u + 3, 3)
                if u == 2:
                    split_weights(i, 0)
                if u == 0 and (not is_static(i) or i >= 1):
                    split_weights(i - 1, 1)

            for g in (2, 3):
                mask_of(2, 2, g)
            tiles_looped(pool, step, 1, 1)
            low(NT - 1, 3)
            pool.wait_ge(multiplied, GROUPS * NT)
            nc.gpsimd.memset(zero_rows[:], 0.0).then_inc(zeroed, 1)
            split_weights(E - 1, 1)
            pool_experts(pool)

        @block.scalar
        def _(act):
            act.dma_start(rw[:], router_w.rearrange("(c p) e -> p c e", p=P)).then_inc(consts_loaded, 16)
            act.dma_start(b1_rows[:], b1.rearrange("e (c p) -> (e c) p", p=P)).then_inc(b1_loaded, 16)
            act.dma_start(rb[:], router_b.rearrange("(o e) -> o e", o=1).broadcast_to([P, E])).then_inc(consts_loaded, 16)
            act.wait_ge(eps_set, 3)

            def ln_root(c):
                act.wait_ge(ln_moments, XCH * (c + 1))
                nc.scalar.activation(sdev[:, c % 2, :], mom[:, c % 2, :, 1], ACT.Sqrt, bias=eps_c[:, 0:1]
                                     ).then_inc(ln_sdev, 1)

            def ln_apply(c):
                act.wait_ge(ln_scale, c + 1)
                if c >= 2:
                    act.wait_ge(cur_ready, c - 1)
                for k in range(XCH // 2):
                    nc.scalar.activation(cur_f[:, c % 2, k, :], x_in[:, c % 4, k, :], ACT.Identity,
                                         bias=nmr[:, c % 2, k:k + 1], scale=rstd[:, c % 2, k:k + 1]).then_inc(cur_f_ready, 1)
                act.wait_ge(cur_f_ready, XCH // 2 * (c + 1))
                act.wait_ge(cur_f_ready_dve, XCH // 2 * (c + 1))
                nc.scalar.activation(cur[:, c * XCH:(c + 1) * XCH, 0, :], cur_f[:, c % 2, :, :], ACT.Copy
                                     ).then_inc(cur_hi_ready, 1)

            def count(t, u, g):
                wait_mask(act, t, g)
                m = mask[:, u % 2, g * GW:(g + 1) * GW]
                nc.scalar.activation(m, m, ACT.Copy, accum_out=cnt4[:, u % 2, g:g + 1]).then_inc(count_ready, 1)

            def sqrt_count(t, u):
                act.wait_ge(cnt_ready, t + 1)
                nc.scalar.activation(root[:, u % 2:u % 2 + 1], cnt[:, u % 2:u % 2 + 1], ACT.Sqrt, bias=eps_head[:, 0:1]
                                     ).then_inc(root_ready, 1)

            def split_hi(t, u, g):
                act.wait_ge(transposed, t * GROUPS + g + 1)
                wait(act, multiplied, t * GROUPS + g - 1)
                nc.scalar.activation(inc_hi[:, g % 2, :], tr_ps[:, g % 2, :], ACT.Copy).then_inc(hi_ready, 1)

            def add_half(t, u):
                b = u % 2
                act.wait_ge(multiplied, (t + 1) * GROUPS)
                act.wait_ge(rdeg_ready, t + 1)
                nc.scalar.activation(part[:, b, :], acc_ps[:, b, D:2 * D], ACT.Copy, scale=rdeg[:, b:b + 1]
                                     ).then_inc(part_ready, 1)

            def root_variance(t, u):
                act.wait_ge(x2_moments, t + 1)
                wait(act, rstd_ready, t)
                nc.scalar.activation(sd_b[:], mom_b[:, 1:2], ACT.Sqrt, bias=eps_row[:, 0:1], scale=X_SCALE ** -2
                                     ).then_inc(sd_ready, 1)

            def high(t, u):
                b = u % 2
                act.wait_ge(xn_ready, t + 1)
                if not is_static(t) or t >= 2:
                    wait(act, xhl_stored[b], (t - b) * 8)
                nc.scalar.activation(xhl[:, b, 0, :], xn[:, b, :], ACT.Copy).then_inc(xhi_ready, 1)

            def copy_transposed(t):
                act.wait_ge(xnT_psum, t + 1)
                nc.scalar.activation(xnT[:].rearrange("p c t -> p (c t)"), ep_ps[:, 0:D], ACT.Copy
                                     ).then_inc(xnT_ready, 1)

            def store(t, u):
                b = u % 2
                act.wait_ge(x2_ready, t + 1)
                act.dma_start(out[bass.ds(t * P, P), :], x2[:, b, :]).then_inc(x2_stored[b], 16)

            def store_input(t, u):
                b = u % 2
                act.wait_ge(xlo_ready, t + 1)
                act.dma_start(xtab[bass.ds(t * P, P), 0:D], xhl[:, b, :, :].rearrange("p h d -> p (h d)").bitcast(U32)
                              ).then_inc(xhl_stored[b], 16)

            def square_weights(e, which, h):
                n = e * 2 + which
                if h == 0:
                    act.wait_ge(w_loaded[which], e * 16 + 16)
                    wait(act, w_total, n)
                wait(act, w_squared, n * 2 + h)
                nc.scalar.activation(w_junk[:], w_in[:, which, h * WH:(h + 1) * WH], ACT.Square,
                                     accum_out=w_sq[:, h:h + 1]).then_inc(w_squared, 1)

            def root_weights(e, which):
                act.wait_ge(w_total, e * 2 + which + 1)
                nc.scalar.activation(w_root[:], w_tot[:], ACT.Sqrt).then_inc(w_rooted, 1)

            def high_weights(e, which, h):
                n = e * 2 + which
                act.wait_ge(w_scaled, n * 2 + h + 1)
                if h == 0:
                    wait(act, w_stored, n * 16)
                cols = slice(h * WH, (h + 1) * WH)
                nc.scalar.activation(w_parts[:, 0, cols], w_in[:, which, cols], ACT.Copy).then_inc(w_hi_ready, 1)

            def weights(u, i, g):
                if u % 2 == 0 and g >= 2 and (u == 2 or not is_static(i) or i >= 1):
                    e, which = (i, 0) if u == 2 else (i - 1, 1)
                    if g == 2:
                        root_weights(e, which)
                    else:
                        high_weights(e, which, 0)
                if u % 2 == 1 and g == 2 and (u == 3 or not is_static(i) or i >= 1):
                    high_weights(i if u == 3 else i - 1, 0 if u == 3 else 1, 1)
                if u % 2 == 1 and g % 2 == 1:
                    square_weights(i, u // 2, g // 2)

            ln_root(0)
            ln_root(1)
            ln_apply(0)
            ln_apply(1)
            for g in range(GROUPS):
                count(0, 0, g)
            sqrt_count(0, 0)
            act.wait_ge(b1_summed, 1)
            nc.scalar.activation(b_norm[:], lg_ps[:, 0:E], ACT.Sqrt).then_inc(b1_rooted, 1)
            ln_root(2)
            ln_apply(2)
            ln_root(3)
            ln_apply(3)

            def step(t, u, i):
                start = is_static(t) and t == 0
                behind = lambda k: not is_static(t) or t >= k
                ahead = lambda k: not is_static(t) or t + k < NT
                for g in range(GROUPS):
                    split_hi(t, u, g)
                    if start and g <= 1:
                        for c in (2 * g + 4, 2 * g + 5):
                            ln_root(c)
                        for c in (2 * g + 4, 2 * g + 5):
                            ln_apply(c)
                    if start and g == 2:
                        for q in range(GROUPS):
                            count(1, 1, q)
                    if g == 0 and behind(1):
                        add_half(t - 1, u - 1)
                        if ahead(1):
                            count(t + 1, u + 1, GROUPS - 1)
                    if g >= 1 and ahead(2) and not start:
                        count(t + 2, u, g - 1)
                    if start and g == 3:
                        for q in range(GROUPS - 1):
                            count(2, 2, q)
                    if g == 1 and behind(2):
                        high(t - 2, u - 2)
                    if g == 2 and ahead(1):
                        sqrt_count(t + 1, u + 1)
                    if g == 2 and behind(1):
                        root_variance(t - 1, u - 1)
                        store(t - 1, u - 1)
                    if g == 2 and behind(2):
                        copy_transposed(t - 2)
                        store_input(t - 2, u - 2)
                    weights(u, i, g)

            tiles_looped(act, step, 1, 1)
            add_half(NT - 1, 3)
            high(NT - 2, 2)
            copy_transposed(NT - 2)
            root_weights(E - 1, 1)
            root_variance(NT - 1, 3)
            high(NT - 1, 3)
            copy_transposed(NT - 1)
            high_weights(E - 1, 1, 0)
            high_weights(E - 1, 1, 1)
            store(NT - 1, 3)
            store_input(NT - 2, 2)
            store_input(NT - 1, 3)
            act_routing(act)
            for b in range(2):
                act.wait_ge(x2_stored[b], 16 * (NT // 2))
                act.wait_ge(xhl_stored[b], 16 * (NT // 2))
            act.sem_inc(rows_stored, 1)
            act_experts(act)

        @block.vector
        def _(dve):
            nc.vector.memset(eps_c[:], LN_EPS).then_inc(eps_set, 1)
            nc.vector.memset(eps_row[:], LN_EPS / X_SCALE ** 2).then_inc(eps_set, 1)
            nc.vector.memset(eps_head[:], HEAD_EPS ** 2).then_inc(eps_set, 1)

            def ln_stats(c):
                dve.wait_ge(x_loaded[c % 4], 16 * (c // 4 + 1))
                for k in range(XCH):
                    nc.vector.bn_stats(stats[:, c % 2, k, :], x_in[:, c % 4, k, :]).then_inc(ln_chain, 1)
                dve.wait_ge(ln_chain, XCH * (c + 1))
                for k in range(XCH):
                    nc.vector.bn_aggr(mom[:, c % 2, k, :], stats[:, c % 2, k, :]).then_inc(ln_moments, 1)

            def ln_norm(c):
                half = XCH // 2
                dve.wait_ge(ln_sdev, c + 1)
                if c >= 2:
                    dve.wait_ge(cur_ready, c - 1)
                nc.vector.reciprocal(rstd[:, c % 2, :], sdev[:, c % 2, :]).then_inc(ln_scale_r, 1)
                dve.wait_ge(ln_scale_r, c + 1)
                nc.vector.scalar_tensor_tensor(nmr[:, c % 2, :], mom[:, c % 2, 0:half, 0], -1.0, rstd[:, c % 2, 0:half],
                                               ALU.mult, ALU.mult).then_inc(ln_scale, 1)
                for k in range(half, XCH):
                    nc.vector.tensor_scalar(cur_f[:, c % 2, k, :], x_in[:, c % 4, k, :], mom[:, c % 2, k, 0:1],
                                            rstd[:, c % 2, k:k + 1], ALU.subtract, ALU.mult).then_inc(cur_f_ready_dve, 1)

            def mask_of(t, u, g):
                if g == 0:
                    dve.wait_ge(adj_loaded[u % 4], (t // 4 + 1) * 16 if is_static(t) else (t - u % 4) * 4 + 16)
                wait(dve, inc_ready, (t - 2) * GROUPS + g + 1)
                nc.vector.tensor_scalar(mask[:, u % 2, g * GW:(g + 1) * GW], adj_t[:, u % 4, g * GW:(g + 1) * GW],
                                        0.0, None, ALU.is_gt).then_inc(mask_ready, 1)

            def head_scale(t, u):
                b = u % 2
                dve.wait_ge(count_ready, (t + 1) * GROUPS)
                nc.vector.tensor_reduce(cnt[:, b:b + 1], cnt4[:, b, :], AX_X, ALU.add).then_inc(cnt_ready, 1)

            def head_scale2(t, u):
                b = u % 2
                dve.wait_ge(root_ready, t + 1)
                nc.vector.reciprocal(rinv[:, b:b + 1], root[:, b:b + 1]).then_inc(rinv_ready, 1)

            def incidence(t, u, g):
                if g == 0:
                    dve.wait_ge(rinv_ready, t + 1)
                a = adj_t[:, u % 4, g * GW:(g + 1) * GW]
                nc.vector.scalar_tensor_tensor(a, mask[:, u % 2, g * GW:(g + 1) * GW], rinv[:, u % 2:u % 2 + 1], a,
                                               ALU.mult, ALU.add, accum_out=deg4[:, u % 2, g:g + 1]).then_inc(inc_ready, 1)

            def degree(t, u):
                b = u % 2
                dve.wait_ge(inc_ready, (t + 1) * GROUPS)
                nc.vector.tensor_reduce(deg[:, b:b + 1], deg4[:, b, :], AX_X, ALU.add).then_inc(deg_ready, 1)

            def degree2(t, u):
                b = u % 2
                dve.wait_ge(deg_ready, t + 1)
                nc.vector.reciprocal(rdeg[:, b:b + 1], deg[:, b:b + 1]).then_inc(rdeg_ready, 1)

            def split_lo(t, u, g):
                dve.wait_ge(hi_ready, t * GROUPS + g + 1)
                nc.vector.tensor_tensor(inc_lo[:, g % 2, :], tr_ps[:, g % 2, :], inc_hi[:, g % 2, :].bitcast(F32),
                                        ALU.subtract).then_inc(lo_ready, 1)

            def residual(t, u):
                b = u % 2
                dve.wait_ge(part_x_ready, t + 1)
                if not is_static(t) or t >= 2:
                    wait(dve, x2_stored[b], (t - b) * 8)
                nc.vector.scalar_tensor_tensor(x2[:, b, :], acc_ps[:, b, 0:D], rdeg[:, b:b + 1], part[:, b, :],
                                               ALU.mult, ALU.add).then_inc(x2_ready, 1)

            def row_stats(t, u):
                dve.wait_ge(x2_ready, t + 1)
                wait(dve, x2_moments, t)
                nc.vector.bn_stats(st_b[:], x2[:, u % 2, :]).then_inc(x2_stats, 1)

            def moments(t):
                nc.vector.bn_aggr(mom_b[:], st_b[:]).then_inc(x2_moments, 1)

            def norm_scale(t):
                dve.wait_ge(sd_ready, t + 1)
                wait(dve, xn_ready, t)
                nc.vector.reciprocal(rstd_b[:], sd_b[:]).then_inc(rstd_ready, 1)

            def normalise(t, u):
                b = u % 2
                dve.wait_ge(rstd_ready, t + 1)
                wait(dve, xnT_psum, t - 1)
                wait(dve, xlo_ready, t - 1)
                nc.vector.tensor_scalar(xn[:, b, :], x2[:, b, :], mom_b[:, 0:1], rstd_b[:, 0:1], ALU.subtract, ALU.mult
                                        ).then_inc(xn_ready, 1)

            def weight_scale(e, which):
                n = e * 2 + which
                dve.wait_ge(w_rooted, n + 1)
                nc.vector.tensor_scalar(w_norm[:, which, bass.ds(e, 1)], w_root[:], TINY, None, ALU.max).then_inc(w_norm_ready, 1)
                nc.vector.tensor_scalar(w_cut[:], w_root[:], TINY, 1.0 / W_TOP, ALU.max, ALU.mult).then_inc(w_cut_ready, 1)
                dve.wait_ge(w_cut_ready, n + 1)
                nc.vector.reciprocal(w_scale[:], w_cut[:]).then_inc(w_scale_ready, 1)

            def scale_weights(e, which, h):
                dve.wait_ge(w_scale_ready, e * 2 + which + 1)
                cols = w_in[:, which, h * WH:(h + 1) * WH]
                nc.vector.tensor_scalar(cols, cols, w_scale[:, 0:1], None, ALU.mult).then_inc(w_scaled, 1)

            def router(t):
                dve.wait_ge(logits_psum, t + 1)
                if is_static(t) and t == 0:
                    dve.wait_ge(consts_loaded, 32)
                lt = logits[:, bass.ds(t, 1), :].rearrange("p o e -> p (o e)")
                nc.vector.scalar_tensor_tensor(lt, lg_ps[:, 0:E], 1.0 / X_SCALE, rb[:], ALU.mult, ALU.add
                                               ).then_inc(logits_ready, 1)

            ln_stats(0)
            ln_stats(1)
            ln_norm(0)
            ln_norm(1)
            dve.wait_ge(b1_turned, 1)
            nc.vector.tensor_copy(b1t[:], ep_ps[:, 0:E * FC].rearrange("p (e c) -> p e c", c=FC)).then_inc(b1_squared, 1)
            dve.wait_ge(b1_squared, 1)
            nc.vector.tensor_tensor(b1_sq[:], b1t[:], b1t[:], ALU.mult).then_inc(b1_squared, 1)
            dve.wait_ge(b1_squared, 2)
            nc.vector.tensor_reduce(b1_sum[:], b1_sq[:], AX_X, ALU.add).then_inc(b1_squared, 1)
            for g in range(GROUPS):
                mask_of(0, 0, g)
            ln_stats(2)
            head_scale(0, 0)
            ln_norm(2)
            ln_stats(3)
            head_scale2(0, 0)
            incidence(0, 0, 0)
            ln_norm(3)
            incidence(0, 0, 1)

            def step(t, u, i):
                start = is_static(t) and t == 0
                behind = lambda k: not is_static(t) or t >= k
                ahead = lambda k: not is_static(t) or t + k < NT
                for g in range(GROUPS):
                    if start and g <= 1:
                        for c in (2 * g + 4, 2 * g + 5):
                            ln_stats(c)
                    split_lo(t, u, g)
                    if start and g <= 1:
                        incidence(t, u, g + 2)
                        for c in (2 * g + 4, 2 * g + 5):
                            ln_norm(c)
                    if start and g == 1:
                        for q in range(GROUPS):
                            mask_of(1, 1, q)
                    if start:
                        if g == 2:
                            mask_of(2, 2, 0)
                            degree(t, u)
                            head_scale(1, 1)
                        if g == 3:
                            head_scale2(1, 1)
                            degree2(t, u)
                            incidence(1, 1, 0)
                            mask_of(2, 2, 1)
                            incidence(1, 1, 1)
                        continue
                    if g == 0:
                        if u == 3 or (u == 1 and (not is_static(i) or i >= 1)):
                            scale_weights(i if u == 3 else i - 1, 0 if u == 3 else 1, 1)
                        incidence(t, u, 2)
                        if behind(3):
                            router(t - 3)
                        if ahead(2):
                            mask_of(t + 2, u + 2, 0)
                    if g == 1:
                        residual(t - 1, u - 1)
                        incidence(t, u, 3)
                        row_stats(t - 1, u - 1)
                        if ahead(2):
                            mask_of(t + 2, u + 2, 1)
                        dve.wait_ge(x2_stats, t)
                        if ahead(1):
                            head_scale(t + 1, u + 1)
                        moments(t - 1)
                    if g == 2:
                        if ahead(1):
                            head_scale2(t + 1, u + 1)
                        degree(t, u)
                        if ahead(1):
                            incidence(t + 1, u + 1, 0)
                        degree2(t, u)
                        norm_scale(t - 1)
                        if u == 2:
                            weight_scale(i, 0)
                        if u == 0:
                            weight_scale(i - 1, 1)
                    if g == 3:
                        if u % 2 == 0:
                            scale_weights(i if u == 2 else i - 1, 0 if u == 2 else 1, 0)
                        if ahead(1):
                            incidence(t + 1, u + 1, 1)
                        normalise(t - 1, u - 1)

            tiles_looped(dve, step, 1, 1)
            top_two(dve, 0, NT - LATE)
            residual(NT - 1, 3)
            row_stats(NT - 1, 3)
            dve.wait_ge(x2_stats, NT)
            moments(NT - 1)
            norm_scale(NT - 1)
            normalise(NT - 1, 3)
            router(NT - 3)
            weight_scale(E - 1, 1)
            scale_weights(E - 1, 1, 0)
            router(NT - 2)
            scale_weights(E - 1, 1, 1)
            router(NT - 1)
            dve_routing(dve)
            dve_experts(dve)

        @block.tensor
        def _(pe):
            pe.wait_ge(ident_set, 2)
            pe.wait_ge(b1_loaded, 16)
            nc.tensor.transpose(ep_ps[:, 0:E * FC], b1_rows[:], ident[0:E * FC, 0:E * FC]).then_inc(b1_turned, 1)
            pe.wait_ge(constants_set, 11)
            pe.wait_ge(b1_squared, 3)
            nc.tensor.matmul(lg_ps[:, 0:E], ones_f[:], b1_sum[:], start=True, stop=True).then_inc(b1_summed, 1)

            def transposes(t, u, g):
                wait(pe, inc_ready, t * GROUPS + g + 1)
                wait(pe, lo_ready, t * GROUPS + g - 1)
                for j in range(GJ):
                    m = nc.tensor.transpose(tr_ps[:, g % 2, j * P:(j + 1) * P],
                                            adj_t[:, u % 4, (g * GJ + j) * P:(g * GJ + j + 1) * P], ident[:])
                m.then_inc(transposed, 1)

            def products(t, u, g):
                wait(pe, lo_ready, t * GROUPS + g + 1)
                if is_static(t) and t == 0:
                    pe.wait_ge(cur_ready, (g + 1) * GJ // XCH)
                if g == 0:
                    wait(pe, x2_ready, t - 1)
                acc = acc_ps[:, u % 2, :]
                for j in range(GJ):
                    jc = g * GJ + j

                    def with_hi():
                        return nc.tensor.matmul(acc, inc_hi[:, g % 2, j * P:(j + 1) * P],
                                                cur[:, jc, :, :].rearrange("p h d -> p (h d)"),
                                                start=(jc == 0), stop=(jc == JC - 1))

                    def with_lo():
                        return nc.tensor.matmul(acc[:, 0:D], inc_lo[:, g % 2, j * P:(j + 1) * P], cur[:, jc, 0, :],
                                                start=False, stop=False)

                    if jc == 0:
                        with_hi()
                        m = with_lo()
                    else:
                        with_lo()
                        m = with_hi()
                m.then_inc(multiplied, 1)

            def epilogue_transpose(t, u):
                pe.wait_ge(xn_ready, t + 1)
                wait(pe, xnT_ready, t)
                for c in range(DC):
                    m = nc.tensor.transpose(ep_ps[:, c * P:(c + 1) * P], xn[:, u % 2, c * P:(c + 1) * P], ident[:])
                m.then_inc(xnT_psum, 1)

            def epilogue_logits(t, u):
                pe.wait_ge(xnT_ready, t + 1)
                if is_static(t) and t == 0:
                    pe.wait_ge(consts_loaded, 32)
                wait(pe, logits_ready, t)
                for c in range(DC):
                    m = nc.tensor.matmul(lg_ps[:, 0:E], xnT[:, c, :], rw[:, c, :], start=(c == 0), stop=(c == DC - 1))
                m.then_inc(logits_psum, 1)

            transposes(0, 0, 0)

            def step(t, u, i):
                for g in range(GROUPS):
                    if g + 1 < GROUPS:
                        transposes(t, u, g + 1)
                    elif not is_static(t) or t + 1 < NT:
                        transposes(t + 1, u + 1, 0)
                    if g == 1 and (not is_static(t) or t >= 2):
                        epilogue_transpose(t - 2, u - 2)
                    if g == 3 and (not is_static(t) or t >= 2):
                        epilogue_logits(t - 2, u - 2)
                    products(t, u, g)

            tiles_looped(pe, step, 1, 1)
            for t in (NT - 2, NT - 1):
                epilogue_transpose(t, t % 4)
                epilogue_logits(t, t % 4)
            pe_routing(pe)
            pe_experts(pe)


_INS = ["x", "adj", "L0_ffn_router_w", "L0_ffn_router_b", "L0_ffn_w1", "L0_ffn_b1", "L0_ffn_w2", "L0_ffn_b2"]


def kernel(**inputs):
    import numpy as _np
    import concourse.bacc as _bacc
    from concourse.bass_utils import run_bass_kernel_spmd as _run

    nc = _bacc.Bacc("TRN2", target_bir_lowering=False, num_devices=1)
    arrays, args = {}, []
    for name in _INS:
        a = _np.ascontiguousarray(inputs[name])
        arrays[f"in_{name}_dram"] = a
        args.append(nc.dram_tensor(f"in_{name}_dram", a.shape, mybir.dt.from_np(a.dtype), kind="ExternalInput").ap())
    n, d = inputs["x"].shape
    args.append(nc.dram_tensor("out_0_dram", (n + PAD_ROWS, d), F32, kind="ExternalOutput").ap())
    gnn_moe_kernel(nc, *args)
    r = _run(nc, [arrays], core_ids=[0])
    return r.results[0]["out_0_dram"][:n]
```
